# Optimizing a Trainium2 kernel written in Bass

```python
import numpy as np
import jax
import jax.numpy as jnp

def _softmax(x, axis=-1):
    return jax.nn.softmax(x, axis=axis)

def _gelu(x):
    return jax.nn.gelu(x, approximate=True)

def _silu(x):
    return jax.nn.silu(x)

def _sigmoid(x):
    return jax.nn.sigmoid(x)

def _layernorm(x, axis=-1, eps=1e-05):
    m = jnp.mean(x, axis=axis, keepdims=True)
    v = jnp.var(x, axis=axis, keepdims=True)
    return (x - m) / jnp.sqrt(v + eps)

def _scatter_add(tgt, idx, src, axis=0):
    return tgt.at[idx].add(src)

def _segment_sum(src, seg, n):
    return jax.ops.segment_sum(src, seg, n)
kernel_name = 'mk_dlrm_tower_d1_rec_r8_ee30da'

def setup_inputs(seed: int=0):
    np.random.seed(seed)
    _w = jnp.asarray

    def _rec_inputs():
        import jax
        import jax.numpy as jnp
        _tk = jax.random.key(seed)
        dense_ctx = jax.random.normal(jax.random.fold_in(_tk, 190), (512, 16), jnp.float32)
        ids = jnp.stack([jax.random.randint(jax.random.fold_in(_tk, 200 + f), (512,), 0, v, jnp.int32) for f, v in enumerate([1250, 1000, 1000, 1000, 1250, 12500, 1250, 12500, 12500, 125000, 12500, 1000, 12500, 1250, 12500, 1000, 125000, 1000, 125000, 1250, 1000, 1000, 1000, 1000, 1000, 1250, 1000, 1000, 1250, 1000, 12500, 1250, 1000, 12500, 1000, 1000, 1000, 1000, 1000])], axis=1)
        tbl_0 = 0.05 * jax.random.normal(jax.random.fold_in(_tk, 500 + 0), (1250, 64), jnp.float32)
        tbl_1 = 0.05 * jax.random.normal(jax.random.fold_in(_tk, 500 + 1), (1000, 64), jnp.float32)
        tbl_2 = 0.05 * jax.random.normal(jax.random.fold_in(_tk, 500 + 2), (1000, 64), jnp.float32)
        tbl_3 = 0.05 * jax.random.normal(jax.random.fold_in(_tk, 500 + 3), (1000, 64), jnp.float32)
        tbl_4 = 0.05 * jax.random.normal(jax.random.fold_in(_tk, 500 + 4), (1250, 64), jnp.float32)
        tbl_5 = 0.05 * jax.random.normal(jax.random.fold_in(_tk, 500 + 5), (12500, 64), jnp.float32)
        tbl_6 = 0.05 * jax.random.normal(jax.random.fold_in(_tk, 500 + 6), (1250, 64), jnp.float32)
        tbl_7 = 0.05 * jax.random.normal(jax.random.fold_in(_tk, 500 + 7), (12500, 64), jnp.float32)
        tbl_8 = 0.05 * jax.random.normal(jax.random.fold_in(_tk, 500 + 8), (12500, 64), jnp.float32)
        tbl_9 = 0.05 * jax.random.normal(jax.random.fold_in(_tk, 500 + 9), (125000, 64), jnp.float32)
        tbl_10 = 0.05 * jax.random.normal(jax.random.fold_in(_tk, 500 + 10), (12500, 64), jnp.float32)
        tbl_11 = 0.05 * jax.random.normal(jax.random.fold_in(_tk, 500 + 11), (1000, 64), jnp.float32)
        tbl_12 = 0.05 * jax.random.normal(jax.random.fold_in(_tk, 500 + 12), (12500, 64), jnp.float32)
        tbl_13 = 0.05 * jax.random.normal(jax.random.fold_in(_tk, 500 + 13), (1250, 64), jnp.float32)
        tbl_14 = 0.05 * jax.random.normal(jax.random.fold_in(_tk, 500 + 14), (12500, 64), jnp.float32)
        tbl_15 = 0.05 * jax.random.normal(jax.random.fold_in(_tk, 500 + 15), (1000, 64), jnp.float32)
        tbl_16 = 0.05 * jax.random.normal(jax.random.fold_in(_tk, 500 + 16), (125000, 64), jnp.float32)
        tbl_17 = 0.05 * jax.random.normal(jax.random.fold_in(_tk, 500 + 17), (1000, 64), jnp.float32)
        tbl_18 = 0.05 * jax.random.normal(jax.random.fold_in(_tk, 500 + 18), (125000, 64), jnp.float32)
        tbl_19 = 0.05 * jax.random.normal(jax.random.fold_in(_tk, 500 + 19), (1250, 64), jnp.float32)
        tbl_20 = 0.05 * jax.random.normal(jax.random.fold_in(_tk, 500 + 20), (1000, 64), jnp.float32)
        tbl_21 = 0.05 * jax.random.normal(jax.random.fold_in(_tk, 500 + 21), (1000, 64), jnp.float32)
        tbl_22 = 0.05 * jax.random.normal(jax.random.fold_in(_tk, 500 + 22), (1000, 64), jnp.float32)
        tbl_23 = 0.05 * jax.random.normal(jax.random.fold_in(_tk, 500 + 23), (1000, 64), jnp.float32)
        tbl_24 = 0.05 * jax.random.normal(jax.random.fold_in(_tk, 500 + 24), (1000, 64), jnp.float32)
        tbl_25 = 0.05 * jax.random.normal(jax.random.fold_in(_tk, 500 + 25), (1250, 64), jnp.float32)
        tbl_26 = 0.05 * jax.random.normal(jax.random.fold_in(_tk, 500 + 26), (1000, 64), jnp.float32)
        tbl_27 = 0.05 * jax.random.normal(jax.random.fold_in(_tk, 500 + 27), (1000, 64), jnp.float32)
        tbl_28 = 0.05 * jax.random.normal(jax.random.fold_in(_tk, 500 + 28), (1250, 64), jnp.float32)
        tbl_29 = 0.05 * jax.random.normal(jax.random.fold_in(_tk, 500 + 29), (1000, 64), jnp.float32)
        tbl_30 = 0.05 * jax.random.normal(jax.random.fold_in(_tk, 500 + 30), (12500, 64), jnp.float32)
        tbl_31 = 0.05 * jax.random.normal(jax.random.fold_in(_tk, 500 + 31), (1250, 64), jnp.float32)
        tbl_32 = 0.05 * jax.random.normal(jax.random.fold_in(_tk, 500 + 32), (1000, 64), jnp.float32)
        tbl_33 = 0.05 * jax.random.normal(jax.random.fold_in(_tk, 500 + 33), (12500, 64), jnp.float32)
        tbl_34 = 0.05 * jax.random.normal(jax.random.fold_in(_tk, 500 + 34), (1000, 64), jnp.float32)
        tbl_35 = 0.05 * jax.random.normal(jax.random.fold_in(_tk, 500 + 35), (1000, 64), jnp.float32)
        tbl_36 = 0.05 * jax.random.normal(jax.random.fold_in(_tk, 500 + 36), (1000, 64), jnp.float32)
        tbl_37 = 0.05 * jax.random.normal(jax.random.fold_in(_tk, 500 + 37), (1000, 64), jnp.float32)
        tbl_38 = 0.05 * jax.random.normal(jax.random.fold_in(_tk, 500 + 38), (1000, 64), jnp.float32)
        _rk = jax.random.fold_in(_tk, 7)
        W_top1 = 0.0606339 * jax.random.normal(jax.random.fold_in(_tk, 801), (272, 512), jnp.float32)
        W_top2 = 0.0441942 * jax.random.normal(jax.random.fold_in(_tk, 802), (512, 256), jnp.float32)
        W_top3 = 0.0625 * jax.random.normal(jax.random.fold_in(_tk, 803), (256, 1), jnp.float32)
        b_top1 = jnp.zeros((512,), jnp.float32)
        b_top2 = jnp.zeros((256,), jnp.float32)
        return (dense_ctx, ids, tbl_0, tbl_1, tbl_2, tbl_3, tbl_4, tbl_5, tbl_6, tbl_7, tbl_8, tbl_9, tbl_10, tbl_11, tbl_12, tbl_13, tbl_14, tbl_15, tbl_16, tbl_17, tbl_18, tbl_19, tbl_20, tbl_21, tbl_22, tbl_23, tbl_24, tbl_25, tbl_26, tbl_27, tbl_28, tbl_29, tbl_30, tbl_31, tbl_32, tbl_33, tbl_34, tbl_35, tbl_36, tbl_37, tbl_38, W_top1, b_top1, W_top2, b_top2, W_top3)
    dense_ctx, ids, tbl_0, tbl_1, tbl_2, tbl_3, tbl_4, tbl_5, tbl_6, tbl_7, tbl_8, tbl_9, tbl_10, tbl_11, tbl_12, tbl_13, tbl_14, tbl_15, tbl_16, tbl_17, tbl_18, tbl_19, tbl_20, tbl_21, tbl_22, tbl_23, tbl_24, tbl_25, tbl_26, tbl_27, tbl_28, tbl_29, tbl_30, tbl_31, tbl_32, tbl_33, tbl_34, tbl_35, tbl_36, tbl_37, tbl_38, W_top1, b_top1, W_top2, b_top2, W_top3 = _rec_inputs()

    def _L0_rec_setup():
        import jax, jax.numpy as jnp
        import numpy as np
        B, M, D = (1024, 39, 64)
        H1, H2 = (128, 128)

        def _cin_forward(x, Ws):
            x0 = x
            h = x
            outs = []
            for W in Ws:
                h = jnp.einsum('bid,bjd,ijh->bhd', x0, h, W)
                outs.append(h)
            out = jnp.concatenate(outs, axis=1)
            return out.sum(axis=-1)
        key = jax.random.key(seed)
        kx, k0, k1 = jax.random.split(key, 3)
        x = jax.random.normal(kx, (B, M, D), dtype=jnp.float32)
        W0 = jax.random.uniform(k0, (M, M, H1), minval=-0.05, maxval=0.05, dtype=jnp.float32)
        W1 = jax.random.uniform(k1, (M, H1, H2), minval=-0.05, maxval=0.05, dtype=jnp.float32)
        return {'x': x, 'W0': W0, 'W1': W1}
    _L0_rec_all = _L0_rec_setup()
    _L0_rec_in = {k: v for k, v in _L0_rec_all.items() if k in ('W0', 'W1')}
    del _L0_rec_all
    return {'dense_ctx': dense_ctx, 'ids': ids, 'tbl_0': tbl_0, 'tbl_1': tbl_1, 'tbl_2': tbl_2, 'tbl_3': tbl_3, 'tbl_4': tbl_4, 'tbl_5': tbl_5, 'tbl_6': tbl_6, 'tbl_7': tbl_7, 'tbl_8': tbl_8, 'tbl_9': tbl_9, 'tbl_10': tbl_10, 'tbl_11': tbl_11, 'tbl_12': tbl_12, 'tbl_13': tbl_13, 'tbl_14': tbl_14, 'tbl_15': tbl_15, 'tbl_16': tbl_16, 'tbl_17': tbl_17, 'tbl_18': tbl_18, 'tbl_19': tbl_19, 'tbl_20': tbl_20, 'tbl_21': tbl_21, 'tbl_22': tbl_22, 'tbl_23': tbl_23, 'tbl_24': tbl_24, 'tbl_25': tbl_25, 'tbl_26': tbl_26, 'tbl_27': tbl_27, 'tbl_28': tbl_28, 'tbl_29': tbl_29, 'tbl_30': tbl_30, 'tbl_31': tbl_31, 'tbl_32': tbl_32, 'tbl_33': tbl_33, 'tbl_34': tbl_34, 'tbl_35': tbl_35, 'tbl_36': tbl_36, 'tbl_37': tbl_37, 'tbl_38': tbl_38, 'W_top1': W_top1, 'b_top1': b_top1, 'W_top2': W_top2, 'b_top2': b_top2, 'W_top3': W_top3, 'L0_rec_W0': _L0_rec_in['W0'], 'L0_rec_W1': _L0_rec_in['W1']}

def reference(dense_ctx, ids, tbl_0, tbl_1, tbl_2, tbl_3, tbl_4, tbl_5, tbl_6, tbl_7, tbl_8, tbl_9, tbl_10, tbl_11, tbl_12, tbl_13, tbl_14, tbl_15, tbl_16, tbl_17, tbl_18, tbl_19, tbl_20, tbl_21, tbl_22, tbl_23, tbl_24, tbl_25, tbl_26, tbl_27, tbl_28, tbl_29, tbl_30, tbl_31, tbl_32, tbl_33, tbl_34, tbl_35, tbl_36, tbl_37, tbl_38, W_top1, b_top1, W_top2, b_top2, W_top3, L0_rec_W0, L0_rec_W1):
    import jax
    import jax.numpy as jnp

    def _L0_rec_ref(x, W0, W1):
        import jax, jax.numpy as jnp
        import numpy as np
        B, M, D = (1024, 39, 64)
        H1, H2 = (128, 128)

        def _cin_forward(x, Ws):
            x0 = x
            h = x
            outs = []
            for W in Ws:
                h = jnp.einsum('bid,bjd,ijh->bhd', x0, h, W)
                outs.append(h)
            out = jnp.concatenate(outs, axis=1)
            return out.sum(axis=-1)
        return _cin_forward(x, (W0, W1))
    e = jnp.stack([tbl_0[ids[:, 0]], tbl_1[ids[:, 1]], tbl_2[ids[:, 2]], tbl_3[ids[:, 3]], tbl_4[ids[:, 4]], tbl_5[ids[:, 5]], tbl_6[ids[:, 6]], tbl_7[ids[:, 7]], tbl_8[ids[:, 8]], tbl_9[ids[:, 9]], tbl_10[ids[:, 10]], tbl_11[ids[:, 11]], tbl_12[ids[:, 12]], tbl_13[ids[:, 13]], tbl_14[ids[:, 14]], tbl_15[ids[:, 15]], tbl_16[ids[:, 16]], tbl_17[ids[:, 17]], tbl_18[ids[:, 18]], tbl_19[ids[:, 19]], tbl_20[ids[:, 20]], tbl_21[ids[:, 21]], tbl_22[ids[:, 22]], tbl_23[ids[:, 23]], tbl_24[ids[:, 24]], tbl_25[ids[:, 25]], tbl_26[ids[:, 26]], tbl_27[ids[:, 27]], tbl_28[ids[:, 28]], tbl_29[ids[:, 29]], tbl_30[ids[:, 30]], tbl_31[ids[:, 31]], tbl_32[ids[:, 32]], tbl_33[ids[:, 33]], tbl_34[ids[:, 34]], tbl_35[ids[:, 35]], tbl_36[ids[:, 36]], tbl_37[ids[:, 37]], tbl_38[ids[:, 38]]], axis=1)
    z = _L0_rec_ref(e, L0_rec_W0, L0_rec_W1)
    z = z.reshape(z.shape[0], -1)
    h = jnp.concatenate([z, dense_ctx], axis=1)
    h = jnp.maximum(h @ W_top1 + b_top1, 0.0)
    h = jnp.maximum(h @ W_top2 + b_top2, 0.0)
    y = h @ W_top3
    return y

_drawn_inputs = setup_inputs


def setup_inputs(seed=0):
    import zlib

    import numpy as np

    out = dict(_drawn_inputs(seed))
    spreads = {'b_top1': (0.0, 0.1), 'b_top2': (0.0, 0.1)}
    factors = {'tbl_0': 4.374,
     'tbl_1': 4.483,
     'tbl_2': 4.226,
     'tbl_3': 4.507,
     'tbl_4': 4.59,
     'tbl_5': 4.5,
     'tbl_6': 4.357,
     'tbl_7': 4.221,
     'tbl_8': 4.461,
     'tbl_9': 4.197,
     'tbl_10': 4.486,
     'tbl_11': 4.309,
     'tbl_12': 4.261,
     'tbl_13': 4.317,
     'tbl_14': 4.367,
     'tbl_15': 4.877,
     'tbl_16': 4.951,
     'tbl_17': 4.54,
     'tbl_18': 4.564,
     'tbl_19': 4.992,
     'tbl_20': 4.817,
     'tbl_21': 4.712,
     'tbl_22': 4.218,
     'tbl_23': 4.396,
     'tbl_24': 4.434,
     'tbl_25': 4.155,
     'tbl_26': 4.547,
     'tbl_27': 4.672,
     'tbl_28': 4.303,
     'tbl_29': 4.28,
     'tbl_30': 4.212,
     'tbl_31': 4.381,
     'tbl_32': 4.692,
     'tbl_33': 4.384,
     'tbl_34': 4.427,
     'tbl_35': 4.581,
     'tbl_36': 4.531,
     'tbl_37': 4.818,
     'tbl_38': 4.562,
     'L0_rec_W1': 8.0}
    for name, (base, spread) in spreads.items():
        noise = np.random.default_rng([zlib.crc32(name.encode()), seed]).standard_normal(out[name].shape)
        drawn = base * np.exp(spread * noise) if base else spread * noise
        out[name] = jnp.asarray(drawn.astype(out[name].dtype))
    for name, factor in factors.items():
        out[name] = (out[name] * factor).astype(out[name].dtype)
    return out
```

```python
FEATURES = 39
DIM = 64
HID = 128
BATCH = 512
BLOCK = 128
BLOCKS = BATCH // BLOCK
HALF = BLOCK // 2
SUB = HALF // 2
WINDOW = 32
GROUP = 8
PAIRS = 400
TOP1 = 512
TOP2 = 256

HALVES = (
    {"X": (0, 7), "M": (7, 6), "Y": (13, 7)},
    {"X": (20, 7), "M": (27, 5), "Y": (32, 7)},
)
FIRST = (0, 20)
COUNT = (20, 19)
SEGMENTS = ("MM", "XX", "XY", "YY", "MX", "MY")


def tri(n, i):
    return i * n - i * (i - 1) // 2


def layout_of_half(half):
    at, start = 0, {}
    for name in SEGMENTS:
        start[name] = at
        n, m = (HALVES[half][g][1] for g in name)
        at += n * (n + 1) // 2 if name[0] == name[1] else n * m
    return start, at


START = [layout_of_half(half)[0] for half in (0, 1)]
ROWS = [layout_of_half(half)[1] for half in (0, 1)]
PAIR_BASE = (0, ROWS[0])

CHUNKS = (
    dict(half=0, lo=0, hi=START[0]["MX"], window=20, own=(0, 0)),
    dict(half=0, lo=START[0]["YY"], hi=ROWS[0], window=7, own=(27, 12)),
    dict(half=1, lo=0, hi=START[1]["MX"], window=0, own=(20, 7)),
    dict(half=1, lo=START[1]["YY"], hi=ROWS[1], window=27, own=(0, 27)),
)
PAIR_ROWS = [c["hi"] - c["lo"] for c in CHUNKS]
CHUNK_ROWS = [c["hi"] - c["lo"] + c["own"][1] for c in CHUNKS]
WRAPPED = 59

MOMENT_TILES = tuple(
    [(3, PAIR_ROWS[3] + 4 * t, 4, 0, 32) for t in range(6)]
    + [(3, PAIR_ROWS[3] + 24, 3, 0, 32)]
    + [(1, PAIR_ROWS[1] + 6 * t, 6, 20, 12) for t in range(2)]
    + [(2, PAIR_ROWS[2], 7, 20, 7)]
)
TILES = len(MOMENT_TILES)


def slot_of(chunk, feature):
    slot = (feature - CHUNKS[chunk]["window"]) % FEATURES
    return slot if slot < WINDOW else None


def group_of(feature):
    half = int(feature >= FIRST[1])
    for name, (first, count) in HALVES[half].items():
        if first <= feature < first + count:
            return half, name, feature - first


def pair_features(half):
    out = []
    for name in SEGMENTS:
        (f, n), (g, m) = (HALVES[half][x] for x in name)
        if name[0] == name[1]:
            out += [(f + i, f + j) for i in range(n) for j in range(i, n)]
        else:
            out += [(f + i, g + j) for i in range(n) for j in range(m)]
    return out


def pieces_of_chunk(chunk):
    c = CHUNKS[chunk]
    out = []
    for name in SEGMENTS:
        row = START[c["half"]][name] - c["lo"]
        if not 0 <= row < PAIR_ROWS[chunk]:
            continue
        (f, n), (g, m) = (HALVES[c["half"]][x] for x in name)
        if name[0] == name[1]:
            out += [(row + tri(n, i), f + i, 1, f + i, n - i) for i in range(n)]
        else:
            out.append((row, f, n, g, m))
    return out


def rows_with(half, name, other):
    group, place = name
    n = HALVES[half][other][1]
    if group == other:
        base = START[half][group * 2]
        out = [(base + tri(n, place), 1, place, n - place)]
        out += [(base + tri(n, j) + place - j, 1, j, 1) for j in range(place)]
    elif group + other in START[half]:
        out = [(START[half][group + other] + place * n, 1, 0, n)]
    else:
        step = HALVES[half][group][1]
        out = [(START[half][other + group] + place, step, 0, n)]
    found = []
    for row, step, first, count in out:
        chunk = 2 * half + int(row >= START[half]["MX"])
        found.append((chunk, row - CHUNKS[chunk]["lo"], step, first, count))
    return found


CROSS = COUNT[0] * COUNT[1]


def extra_of(i):
    half, group, _ = group_of(i)
    if group == "Y":
        return 0, START[half]["YY"]
    if group == "X":
        return START[half]["MX"], ROWS[half] - START[half]["MX"]
    return None


def additions_of(i):
    half, group, place = group_of(i)
    other = 1 - half
    out = []
    for g, (first, _) in HALVES[half].items():
        for chunk, row, step, at, count in rows_with(half, (group, place), g):
            a = first + at - FIRST[half]
            if half == 0:
                source, steps = a * COUNT[1], (COUNT[1], 1)
            else:
                source, steps = a, (1, COUNT[1])
            out.append((source, [(steps[0], count), (steps[1], COUNT[other])],
                        chunk, slot_of(chunk, FIRST[other]), row, [(0, step), (1, 0)]))
    x, m, y = (HALVES[half][g] for g in "XMY")
    start = START[half]
    one, two = 2 * half, 2 * half + 1
    if group == "Y":
        for j in range(m[1]):
            out.append((CROSS + start["MM"] + tri(m[1], j), [(1, m[1] - j)],
                        two, slot_of(two, m[0] + j), start["MY"] - CHUNKS[two]["lo"] + j * y[1] + place, [(1, 0)]))
        for j in range(x[1]):
            out.append((CROSS + start["XX"] + tri(x[1], j), [(1, x[1] - j)],
                        one, slot_of(one, x[0] + j), start["XY"] + j * y[1] + place, [(1, 0)]))
        for chunk, row, step, at, count in rows_with(half, ("Y", place), "Y"):
            out.append((CROSS + start["XY"] + at, [(y[1], x[1]), (1, count)],
                        chunk, slot_of(chunk, x[0]), row, [(1, 0), (0, step)]))
    if group == "X":
        extra = CROSS - start["MX"]
        for chunk, row, step, at, count in rows_with(half, ("X", place), "X"):
            out.append((extra + start["MX"] + at, [(x[1], m[1]), (1, count)],
                        chunk, slot_of(chunk, m[0]), row, [(1, 0), (0, step)]))
        out.append((extra + start["MY"], [(y[1], m[1]), (1, y[1])],
                    one, slot_of(one, m[0]), start["XY"] + place * y[1], [(1, 0), (0, 1)]))
    return out


def build(nc, args):
    import concourse.bass as bass
    from concourse import mybir
    from contextlib import ExitStack

    FP = mybir.dt.float32
    ALU = mybir.AluOpType
    ACT = mybir.ActivationFunctionType

    ctx = ExitStack()
    with ctx:
        def sb(name, shape, dt=FP):
            return ctx.enter_context(nc.sbuf_tensor(name, shape, dt))

        def sem(name):
            return ctx.enter_context(nc.semaphore(name))

        SLOTS = len(CHUNKS) * WINDOW
        shared = sb("shared", [128, SLOTS * 128])
        weights_h = shared[:, :].rearrange("h (s r) -> h s r", r=128)
        products = [shared[:, n * 4096:(n + 1) * 4096].rearrange("p (b r) -> p b r", r=128) for n in range(2)]
        moments = [shared[:, (2 + n) * 4096:(3 + n) * 4096].rearrange("r (c q) -> r c q", c=WINDOW) for n in range(2)]
        weights = sb("weights", [128, SLOTS, 128])
        pair_w = [weights[:, 8 * n:8 * n + 7, :] for n in range(2)]
        pair_sum = weights[:, 16:23, :]
        w1 = sb("w1", [128, FEATURES * 128])
        z1_w = w1[:, 0:TILES * 128].rearrange("p (t h) -> p t h", h=128)
        z1_w2 = w1[:, TILES * 128:2 * TILES * 128].rearrange("p (t h) -> p t h", h=128)
        second = w1[:, 2 * TILES * 128:3 * TILES * 128].rearrange("p (t s) -> p t s", s=128)
        z = w1[:, 3 * TILES * 128:3 * TILES * 128 + 2 * BATCH]
        rows_in = sb("rows_in", [128, (FEATURES + 2) * DIM])
        xt_all = sb("xt", [128, 2 * FEATURES * HALF])
        xt = [xt_all[:, n * FEATURES * HALF:(n + 1) * FEATURES * HALF].rearrange("p (f b) -> p f b", b=HALF) for n in (0, 1)]
        pair_t = xt_all[:, FEATURES * HALF:FEATURES * HALF + PAIRS + CROSS]
        xd = sb("xd", [128, HALF, 2, WRAPPED])
        ids_now = sb("ids_now", [128, FEATURES], mybir.dt.int32)
        gate = sb("gate", [128, 2])
        ident = sb("ident", [128, 128])
        top1_w = rows_in[:, 0:2 * TOP1].rearrange("p (t n) -> p t n", n=TOP1)
        top1_wd = rows_in[0:16, 2 * TOP1:2 * TOP1 + TOP1]
        top2_w = rows_in[:, 3 * TOP1:3 * TOP1 + 4 * TOP2].rearrange("p (t n) -> p t n", n=TOP2)
        hidden1 = xt_all[:, 0:4 * BATCH].rearrange("p (t s) -> p t s", s=BATCH)
        xd_flat = xd[:, :, :, :].rearrange("p b q f -> p (b q f)")
        hidden2 = xd_flat[:, 0:2 * BATCH].rearrange("p (t s) -> p t s", s=BATCH)
        dense = xd_flat[0:16, 2 * BATCH:3 * BATCH]
        answer = xd_flat[0:1, 3 * BATCH:4 * BATCH]
        columns = xd_flat[:, 4 * BATCH:4 * BATCH + 8]
        bank = [ctx.enter_context(nc.psum_tensor(f"bank{n}", [128, 512], FP)) for n in range(8)]
        ring, flip, z2_bank, z1_bank = bank[0:4], bank[4:6], bank[6], bank[7]

        w0_loaded = sem("w0_loaded")
        w1_loaded = sem("w1_loaded")
        ids_loaded = sem("ids_loaded")
        z1w_loaded = sem("z1w_loaded")
        top_loaded = sem("top_loaded")
        second_loaded = [sem(f"second_loaded{c}") for c in range(4)]
        answer_stored = sem("answer_stored")
        ident_set = sem("ident_set")
        gate_passed = sem("gate_passed")
        edges_zeroed = sem("edges_zeroed")
        xd_zeroed = sem("xd_zeroed")
        places_zeroed = sem("places_zeroed")
        gathered = sem("gathered")
        pairs_summed = sem("pairs_summed")
        pairs_flipped = sem("pairs_flipped")
        pairs_ready = sem("pairs_ready")
        direct_a = sem("direct_a")
        direct_b = sem("direct_b")
        placed_a = sem("placed_a")
        placed_b = sem("placed_b")
        extra_done = sem("extra_done")
        added = sem("added")
        turned = sem("turned")
        kept_act = sem("kept_act")
        kept_dve = sem("kept_dve")
        flipped = sem("flipped")
        flip_freed = sem("flip_freed")
        xd_ready = sem("xd_ready")
        products_ready = sem("products_ready")
        moments_out = sem("moments_out")
        moments_ready = sem("moments_ready")
        moments_freed = sem("moments_freed")
        z1w_ready = sem("z1w_ready")
        z1_done = sem("z1_done")
        z_kept = sem("z_kept")
        top_done = sem("top_done")
        top_kept = sem("top_kept")

        CHUNK_TILES = [sum(t[0] == chunk for t in MOMENT_TILES) for chunk in range(4)]
        C_BANKS = SLOTS // 4
        FLIP_BANKS = 10
        GROUPS = HALF // GROUP
        SUB_GROUPS = GROUPS // 2
        BLOCK_GROUPS = len(CHUNKS) * GROUPS
        RING = len(ring)
        FREE_GROUPS = 2 * SUB_GROUPS

        def place_direct(op, tail, i, half, done):
            source = bank[4 * half + i % 4]
            moves = []
            one, two = 2 * half, 2 * half + 1
            if slot_of(one, i) is not None:
                moves.append((one, 0, START[half]["MX"]))
            if slot_of(two, i) is not None:
                own_y = group_of(i)[:2] == (half, "Y")
                moves.append((two, START[half]["YY" if own_y else "MX"], ROWS[half]))
            for n, (chunk, lo, hi) in enumerate(moves):
                row = lo - CHUNKS[chunk]["lo"]
                ins = op(weights_h[:, WINDOW * chunk + slot_of(chunk, i), row:row + hi - lo],
                         source[:, lo:hi], *tail)
                if n == len(moves) - 1:
                    ins.then_inc(done, 1)

        def ap_of(base, offset, axes):
            return bass.AP(base.tensor, base.offset + offset, [list(base.ap[0])] + [list(a) for a in axes])

        block = ctx.enter_context(nc.Block())

        @block.sync
        def _(sp):
            sp.dma_start(pair_w[0], args["pairs_a"].rearrange("(t p) h -> p t h", p=128)).then_inc(w0_loaded, 16)
            sp.dma_start(pair_w[1], args["pairs_b"].rearrange("(t p) h -> p t h", p=128)).then_inc(w0_loaded, 16)
            sp.dma_start(w1[:, :], args["w1"]).then_inc(w1_loaded, 16)
            sp.wait_ge(extra_done, FEATURES)
            sp.dma_start(z1_w, args["z1_a"].rearrange("t p h -> p t h")).then_inc(z1w_loaded, 16)
            sp.dma_start(z1_w2, args["z1_b"].rearrange("t p h -> p t h")).then_inc(z1w_loaded, 16)
            with sp.Fori(0, BLOCKS) as k:
                sp.wait_ge(z_kept, 2 * (k + 1))
                for chunk in (1, 2, 3):
                    sp.wait_ge(moments_ready, RING + BLOCK_GROUPS * k + GROUPS * (chunk + 1))
                    for t, (of, row, n, slot, slots) in enumerate(MOMENT_TILES):
                        if of == chunk:
                            src = moments[chunk % 2][row:row + n, slot:slot + slots, :]
                            sp.dma_start(second[0:n * slots, t, :], src).then_inc(second_loaded[chunk], 16)
            sp.wait_ge(flipped, 1 + FLIP_BANKS * BLOCKS)
            sp.dma_start(top1_w, args["W_top1"][0:256, :].rearrange("(t p) n -> p t n", p=128)).then_inc(top_loaded, 16)
            sp.dma_start(top1_wd, args["W_top1"][256:272, :]).then_inc(top_loaded, 16)
            sp.dma_start(top2_w, args["W_top2"].rearrange("(t p) n -> p t n", p=128)).then_inc(top_loaded, 16)
            sp.wait_ge(moments_out, FREE_GROUPS + BLOCK_GROUPS * BLOCKS)
            sp.dma_start(dense, args["dense_t"]).then_inc(top_loaded, 16)
            sp.dma_start(columns, args["columns"]).then_inc(top_loaded, 16)
            sp.wait_ge(top_kept, 7)
            sp.dma_start(args["out"].rearrange("s o -> o s"), answer).then_inc(answer_stored, 16)
            sp.wait_ge(answer_stored, 16)

        @block.gpsimd
        def _(pool):
            pool.memset(rows_in[:, 0:DIM], 0.0).then_inc(edges_zeroed, 1)
            pool.memset(rows_in[:, (FEATURES + 1) * DIM:], 0.0).then_inc(flipped, 1)
            pool.memset(gate[:, :], 0.0).then_inc(gate_passed, 1)
            pool.memset(ident[:, :], 1.0).then_inc(ident_set, 1)
            pool.wait_ge(ident_set, 1)
            pool.affine_select(out=ident[:, :], in_=ident[:, :], compare_op=ALU.is_equal, fill=0.0,
                               base=0, pattern=[[-1, 128]], channel_multiplier=1).then_inc(ident_set, 1)
            with pool.Fori(0, BLOCKS) as k:
                pool.wait_ge(gate_passed, k + 1)
                pool.wait_ge(flipped, 1 + FLIP_BANKS * k)
                pool.dma_start(ids_now[:, :], args["ids"][bass.ts(k, BLOCK), :]).then_inc(ids_loaded, 16)
                pool.wait_ge(ids_loaded, 16 * (k + 1))
                pool.tensor_tensor(gate[:, 1:2], gate[:, 0:1], gate[:, 0:1], ALU.add).then_inc(gate_passed, 1)
                for f in range(FEATURES):
                    pool.indirect_dma_start(
                        rows_in[:, (f + 1) * DIM:(f + 2) * DIM], None, args[f"tbl_{f}"],
                        bass.IndirectOffsetOnAxis(ap=ids_now[:, f:f + 1], axis=0)).then_inc(gathered, 16)

        @block.scalar
        def _(act):
            for n, width in enumerate((512, PAIRS + CROSS - 512)):
                act.wait_ge(pairs_flipped, n + 1)
                act.activation(pair_t[:, 512 * n:512 * n + width], ring[n][:, 0:width], ACT.Copy).then_inc(pairs_ready, 1)
            act.wait_ge(places_zeroed, 1)
            for i in range(FEATURES):
                act.wait_ge(direct_a, i + 1)
                place_direct(act.activation, (ACT.Copy,), i, 0, placed_a)

            def flip_out(k):
                at = FEATURES * HALF * (k % 2)
                for j in range(FLIP_BANKS):
                    act.wait_ge(flipped, 1 + FLIP_BANKS * k + j + 1)
                    tiles = flip[j % 2][:, :].rearrange("p (t s) -> p t s", s=BLOCK)
                    low, high = int(j == 0), 3 if j == FLIP_BANKS - 1 else 4
                    for part, lo, hi, f, of in ((0, low, 4, 4 * j - 1 + low, 0), (64, 0, high, 4 * j, HALF)):
                        out = xt_all[part:part + 64, bass.ds(at + HALF * f, HALF * (hi - lo))]
                        last = act.activation(out.rearrange("p (t s) -> p t s", s=HALF),
                                              tiles[part:part + 64, lo:hi, of:of + HALF], ACT.Copy)
                    last.then_inc(flip_freed, 1)

            def spread(k):
                at = FEATURES * HALF * (k % 2)
                act.wait_ge(flip_freed, FLIP_BANKS * (k + 1))
                for f, to, n in ((20, 20, 19), (0, 39, 13), (0, 0, 20), (13, 52, 7)):
                    for q in range(2):
                        part = slice(64 * q, 64 * q + 64)
                        rows = xt_all[part, bass.ds(at + HALF * f, HALF * n)].rearrange("p (f b) -> p b f", b=HALF)
                        last = act.activation(xd[part, :, q, to:to + n], rows, ACT.Copy)
                    last.then_inc(xd_ready, 1)

            flip_out(0)
            act.wait_ge(xd_zeroed, 1)
            spread(0)
            for v in range(0, C_BANKS, 2):
                act.wait_ge(turned, v + 1)
                act.activation(weights[:, 4 * v:4 * v + 4, :].rearrange("r s h -> r (s h)"),
                               ring[v % 4][:, :], ACT.Copy).then_inc(kept_act, 1)

            def chunk_out(k, chunk):
                act.wait_ge(moments_freed, 4 * k + chunk + 1)
                if chunk == 3:
                    act.wait_ge(second_loaded[1], 16 * CHUNK_TILES[1] * (k + 1))
                n = CHUNK_ROWS[chunk]
                out = moments[chunk % 2].rearrange("r c (q b) -> r c q b", q=2)
                for g in range(GROUPS):
                    act.wait_ge(moments_out, FREE_GROUPS + BLOCK_GROUPS * k + GROUPS * chunk + g + 1)
                    act.activation(out[0:n, :, :, GROUP * g:GROUP * (g + 1)],
                                   ring[g % 4][0:n, :].rearrange("r (b q c) -> r c q b", b=GROUP, q=2),
                                   ACT.Copy).then_inc(moments_ready, 1)

            def block_out(k, last):
                chunk_out(k, 1)
                chunk_out(k, 2)
                if not last:
                    act.wait_ge(products_ready, 8 * k + 1)
                    flip_out(k + 1)
                chunk_out(k, 3)
                if not last:
                    act.wait_ge(moments_out, FREE_GROUPS + BLOCK_GROUPS * (k + 1))
                    spread(k + 1)
                    act.wait_ge(second_loaded[2], 16 * CHUNK_TILES[2] * (k + 1))
                    chunk_out(k + 1, 0)
                act.wait_ge(moments_freed, 2 + 4 * (k + 1))
                act.activation(z[:, bass.ds(BATCH + BLOCK * k, BLOCK)], z2_bank[:, 0:BLOCK], ACT.Copy).then_inc(z_kept, 1)
                act.wait_ge(z1_done, k + 1)
                act.activation(z[:, bass.ds(BLOCK * k, BLOCK)], z1_bank[:, 0:BLOCK], ACT.Copy).then_inc(z_kept, 1)

            chunk_out(0, 0)
            with act.Fori(0, BLOCKS - 1) as k:
                block_out(k, False)
            block_out(BLOCKS - 1, True)
            act.wait_ge(top_loaded, 80)
            for t in range(4):
                act.wait_ge(top_done, t + 1)
                act.activation(hidden1[:, t, :], ring[t][:, :], ACT.Relu, bias=columns[:, t:t + 1]).then_inc(top_kept, 1)
            for t in range(2):
                act.wait_ge(top_done, t + 5)
                act.activation(hidden2[:, t, :], flip[t][:, :], ACT.Relu, bias=columns[:, 4 + t:5 + t]).then_inc(top_kept, 1)
            act.wait_ge(top_done, 7)
            act.activation(answer, z1_bank[0:1, :], ACT.Copy).then_inc(top_kept, 1)

        @block.vector
        def _(dve):
            for chunk in range(4):
                nc.vector.memset(weights_h[:, WINDOW * chunk:WINDOW * (chunk + 1), PAIR_ROWS[chunk]:], 0.0)
            for half in (0, 1):
                two = 2 * half + 1
                first = slot_of(two, HALVES[half]["Y"][0])
                yy = START[half]["MX"] - START[half]["YY"]
                for lo, hi in ((0, first), (first + 7, WINDOW)):
                    if hi > lo:
                        last = nc.vector.memset(weights_h[:, WINDOW * two + lo:WINDOW * two + hi, 0:yy], 0.0)
            last.then_inc(places_zeroed, 1)
            dve.wait_ge(w0_loaded, 32)
            nc.vector.tensor_tensor(pair_sum, pair_w[0], pair_w[1], ALU.add).then_inc(pairs_summed, 1)
            nc.vector.memset(xd[:, :, :, :].rearrange("p b q f -> p (b q f)"), 0.0).then_inc(xd_zeroed, 1)
            for i in range(FEATURES):
                dve.wait_ge(direct_b, i + 1)
                place_direct(nc.vector.tensor_copy, (), i, 1, placed_b)
            dve.wait_ge(placed_a, FEATURES)
            for i in range(FEATURES):
                dve.wait_ge(extra_done, i + 1)
                if i:
                    dve.wait_ge(added, i)
                else:
                    dve.wait_ge(placed_b, FEATURES)
                moves = additions_of(i)
                for n, (col, axes, chunk, slot, row, steps) in enumerate(moves):
                    source = ap_of(ring[i % 4][:, :], col, axes)
                    place = ap_of(shared[:, :], (WINDOW * chunk + slot) * 128 + row,
                                  [(128 * s + r, count) for (s, r), (_, count) in zip(steps, axes)])
                    ins = nc.vector.tensor_tensor(place, source, place, ALU.add)
                ins.then_inc(added, 1)
            for v in range(1, C_BANKS, 2):
                dve.wait_ge(turned, v + 1)
                nc.vector.tensor_copy(weights[:, 4 * v:4 * v + 4, :].rearrange("r s h -> r (s h)"),
                                      ring[v % 4][:, :]).then_inc(kept_dve, 1)
            dve.wait_ge(z1w_loaded, 32)
            nc.vector.tensor_tensor(z1_w, z1_w, z1_w2, ALU.add).then_inc(z1w_ready, 1)

            def multiply(k, x):
                dve.wait_ge(flip_freed, FLIP_BANKS * (k + 1))
                for chunk in range(4):
                    for s in range(2):
                        dve.wait_ge(moments_out, SUB_GROUPS * (8 * k + 2 * chunk + s + 1))
                        b = slice(SUB * s, SUB * (s + 1))
                        own, count = CHUNKS[chunk]["own"]
                        if count:
                            row = PAIR_ROWS[chunk]
                            nc.vector.tensor_copy(products[s][:, :, row:row + count],
                                                  x[:, own:own + count, b].rearrange("p f b -> p b f"))
                        for row, fa, na, fb, nb in pieces_of_chunk(chunk):
                            out = products[s][:, :, row:row + na * nb].rearrange("p b (i j) -> p b i j", i=na)
                            one, two = x[:, fa:fa + na, b], x[:, fb:fb + nb, b]
                            one = one.rearrange("p (f o) b -> p b f o", o=1).to_broadcast([128, SUB, na, nb])
                            two = two.rearrange("p (o f) b -> p b o f", o=1).to_broadcast([128, SUB, na, nb])
                            last = nc.vector.tensor_tensor(out, one, two, ALU.mult)
                        last.then_inc(products_ready, 1)

            with dve.Fori(0, BLOCKS // 2) as two_blocks:
                multiply(2 * two_blocks, xt[0])
                multiply(2 * two_blocks + 1, xt[1])

        @block.tensor
        def _(pe):
            pe.wait_ge(ident_set, 2)
            pe.wait_ge(pairs_summed, 1)
            for t in range(7):
                n = min(128, PAIRS + CROSS - 128 * t)
                last = nc.tensor.transpose(ring[t // 4][:, 128 * (t % 4):128 * (t % 4) + n],
                                           pair_sum[0:n, t, :], ident[0:n, 0:n])
                if t in (3, 6):
                    last.then_inc(pairs_flipped, 1)
            pe.wait_ge(pairs_ready, 2)
            pe.wait_ge(w1_loaded, 16)
            for i in range(FEATURES):
                for half, placed, done in ((0, placed_a, direct_a), (1, placed_b, direct_b)):
                    if i >= 4:
                        pe.wait_ge(placed, i - 3)
                    col = PAIR_BASE[half]
                    nc.tensor.matmul(bank[4 * half + i % 4][:, 0:ROWS[half]], w1[:, 128 * i:128 * (i + 1)],
                                     pair_t[:, col:col + ROWS[half]], start=True, stop=True).then_inc(done, 1)

            def flip_bank(k, j):
                if j == 0:
                    pe.wait_ge(gathered, 16 * FEATURES * (k + 1))
                for t in range(4 * j, 4 * j + 4):
                    last = nc.tensor.transpose(flip[j % 2][:, BLOCK * (t % 4):BLOCK * (t % 4 + 1)],
                                               rows_in[:, DIM * t:DIM * (t + 2)], ident[:, :])
                return last

            pe.wait_ge(placed_a, FEATURES)
            pe.wait_ge(placed_b, FEATURES)
            for i in range(FEATURES):
                if i >= 4:
                    pe.wait_ge(added, i - 3)
                extra = extra_of(i)
                w = w1[:, 128 * i:128 * (i + 1)]
                last = nc.tensor.matmul(ring[i % 4][:, 0:CROSS], w, pair_t[:, PAIRS:], start=True, stop=True)
                if extra:
                    col = PAIR_BASE[group_of(i)[0]] + extra[0]
                    last = nc.tensor.matmul(ring[i % 4][:, CROSS:CROSS + extra[1]], w, pair_t[:, col:col + extra[1]],
                                            start=True, stop=True)
                last.then_inc(extra_done, 1)
                if i == FEATURES // 2:
                    pe.wait_ge(edges_zeroed, 1)
                    for j in range(FLIP_BANKS):
                        if j >= 2:
                            pe.wait_ge(flip_freed, j - 1)
                        flip_bank(0, j).then_inc(flipped, 1)
            pe.wait_ge(added, FEATURES)
            for v in range(C_BANKS):
                if v >= 4:
                    pe.wait_ge(kept_dve if v % 2 else kept_act, v // 2 - 1)
                for s in range(4 * v, 4 * v + 4):
                    last = nc.tensor.transpose(ring[v % 4][:, 128 * (s % 4):128 * (s % 4 + 1)], weights_h[:, s, :], ident[:, :])
                last.then_inc(turned, 1)
            pe.wait_ge(kept_act, C_BANKS // 2)
            pe.wait_ge(kept_dve, C_BANKS // 2)
            nc.tensor.matmul(z1_bank[0:1, 0:1], ident[:, 0:1], ident[:, 0:1], start=True, stop=True).then_inc(moments_out, FREE_GROUPS)
            nc.tensor.matmul(z1_bank[0:1, 0:1], ident[:, 0:1], ident[:, 0:1], start=True, stop=True).then_inc(moments_freed, 2)
            nc.tensor.matmul(z1_bank[0:1, 0:1], ident[:, 0:1], ident[:, 0:1], start=True, stop=True).then_inc(moments_ready, RING)
            nc.tensor.matmul(z1_bank[0:1, 0:1], ident[:, 0:1], ident[:, 0:1], start=True, stop=True).then_inc(z_kept, 2)
            pe.wait_ge(z1w_ready, 1)

            def take_moments(k, chunk):
                n, window = CHUNK_ROWS[chunk], CHUNKS[chunk]["window"]
                for g in range(GROUPS):
                    s, q = divmod(g, SUB_GROUPS)
                    if q == 0:
                        pe.wait_ge(products_ready, 8 * k + 2 * chunk + s + 1)
                    pe.wait_ge(moments_ready, BLOCK_GROUPS * k + GROUPS * chunk + g + 1)
                    for j in range(GROUP):
                        out = ring[g % 4][0:n, 64 * j:64 * (j + 1)].rearrange("r (q c) -> r q c", q=2)
                        last = nc.tensor.matmul(out, products[s][:, GROUP * q + j, 0:n],
                                                xd[:, GROUP * g + j, :, window:window + WINDOW], start=True, stop=True)
                    last.then_inc(moments_out, 1)

            def weigh(k, chunk, flips):
                n = CHUNK_ROWS[chunk]
                pe.wait_ge(moments_ready, RING + BLOCK_GROUPS * k + GROUPS * (chunk + 1))
                if chunk == 0:
                    pe.wait_ge(z_kept, 2 * (k + 1))
                for c in range(WINDOW):
                    last = nc.tensor.matmul(z2_bank[:, 0:BLOCK], weights[0:n, WINDOW * chunk + c, :],
                                            moments[chunk % 2][0:n, c, :],
                                            start=(chunk == 0 and c == 0), stop=(chunk == 3 and c == WINDOW - 1))
                    if flips and c % 3 == 1 and c // 3 < FLIP_BANKS:
                        j = c // 3
                        pe.wait_ge(flip_freed, FLIP_BANKS * (k + 1) + j - 1)
                        flip_bank(k + 1, j).then_inc(flipped, 1)
                last.then_inc(moments_freed, 1)

            def whole_block(k, last_one):
                pe.wait_ge(xd_ready, 4 * (k + 1))
                take_moments(k, 1)
                weigh(k, 0, False)
                take_moments(k, 2)
                weigh(k, 1, not last_one)
                take_moments(k, 3)
                weigh(k, 2, False)
                if not last_one:
                    pe.wait_ge(xd_ready, 4 * (k + 1) + 2)
                    take_moments(k + 1, 0)
                weigh(k, 3, False)
                for chunk in (1, 2, 3):
                    pe.wait_ge(second_loaded[chunk], 16 * CHUNK_TILES[chunk] * (k + 1))
                for t, (_, _, n, _, slots) in enumerate(MOMENT_TILES):
                    last = nc.tensor.matmul(z1_bank[:, 0:BLOCK], z1_w[0:n * slots, t, :], second[0:n * slots, t, :],
                                            start=(t == 0), stop=(t == TILES - 1))
                last.then_inc(z1_done, 1)

            pe.wait_ge(xd_ready, 2)
            take_moments(0, 0)
            with pe.Fori(0, BLOCKS - 1) as k:
                whole_block(k, False)
            whole_block(BLOCKS - 1, True)
            pe.wait_ge(top_loaded, 80)
            pe.wait_ge(z_kept, 2 + 2 * BLOCKS)
            for t in range(4):
                cols = slice(128 * t, 128 * (t + 1))
                nc.tensor.matmul(ring[t][:, :], top1_w[:, 0, cols], z[:, 0:BATCH], start=True, stop=False)
                nc.tensor.matmul(ring[t][:, :], top1_w[:, 1, cols], z[:, BATCH:2 * BATCH], start=False, stop=False)
                nc.tensor.matmul(ring[t][:, :], top1_wd[:, cols], dense, start=False, stop=True).then_inc(top_done, 1)
            pe.wait_ge(top_kept, 4)
            for t in range(2):
                for s in range(4):
                    last = nc.tensor.matmul(flip[t][:, :], top2_w[:, s, 128 * t:128 * (t + 1)], hidden1[:, s, :],
                                            start=(s == 0), stop=(s == 3))
                last.then_inc(top_done, 1)
            pe.wait_ge(top_kept, 6)
            for s in range(2):
                last = nc.tensor.matmul(z1_bank[0:1, :], columns[:, 6 + s:7 + s], hidden2[:, s, :], start=(s == 0), stop=(s == 1))
            last.then_inc(top_done, 1)


def pair_index():
    zero = FEATURES * FEATURES
    pairs = pair_features(0) + pair_features(1)
    pairs += [(a, b) for a in range(COUNT[0]) for b in range(FIRST[1], FEATURES)]
    one = [a * FEATURES + b for a, b in pairs]
    two = [b * FEATURES + a if a != b else zero for a, b in pairs]
    fill = [zero] * (-len(pairs) % 128)
    return one + fill, two + fill


def moment_index():
    zero = FEATURES * FEATURES
    one, two = [], []
    for chunk, row, n, slot, slots in MOMENT_TILES:
        rows_one, rows_two = [], []
        for r in range(row, row + n):
            x = CHUNKS[chunk]["own"][0] + r - PAIR_ROWS[chunk]
            for s in range(slot, slot + slots):
                f = (CHUNKS[chunk]["window"] + s) % FEATURES
                rows_one.append(x * FEATURES + f)
                both = chunk == 3 and not (x < FIRST[1] and f < FIRST[1])
                rows_two.append(f * FEATURES + x if both else zero)
        fill = [zero] * (128 - n * slots)
        one += rows_one + fill
        two += rows_two + fill
    return one, two


def kernel(**inputs):
    import numpy as np
    import concourse.bacc as bacc
    from concourse import mybir
    from concourse.bass_utils import run_bass_kernel_spmd as run

    nc = bacc.Bacc("TRN2", target_bir_lowering=False, num_devices=1)
    w0 = np.asarray(inputs["L0_rec_W0"]).reshape(FEATURES * FEATURES, HID)
    w0 = np.concatenate([w0, np.zeros((1, HID), w0.dtype)])
    pairs_a, pairs_b = pair_index()
    z1_a, z1_b = moment_index()
    arrays = {
        "ids": inputs["ids"],
        "pairs_a": w0[np.array(pairs_a)],
        "pairs_b": w0[np.array(pairs_b)],
        "z1_a": w0[np.array(z1_a)].reshape(TILES, 128, HID),
        "z1_b": w0[np.array(z1_b)].reshape(TILES, 128, HID),
        "w1": np.asarray(inputs["L0_rec_W1"]).transpose(1, 0, 2).reshape(HID, FEATURES * HID),
        "dense_t": np.asarray(inputs["dense_ctx"]).T,
        "W_top1": inputs["W_top1"],
        "W_top2": inputs["W_top2"],
        "columns": np.concatenate([np.asarray(inputs[n]).reshape(-1, 128) for n in ("b_top1", "b_top2", "W_top3")]).T,
    }
    arrays.update({f"tbl_{f}": inputs[f"tbl_{f}"] for f in range(FEATURES)})
    arrays = {f"in_{n}": np.ascontiguousarray(a) for n, a in arrays.items()}
    args = {n[3:]: nc.dram_tensor(n, a.shape, mybir.dt.from_np(a.dtype), kind="ExternalInput").ap()
            for n, a in arrays.items()}
    args["out"] = nc.dram_tensor("out", (BATCH, 1), mybir.dt.float32, kind="ExternalOutput").ap()
    build(nc, args)
    return run(nc, [arrays], core_ids=[0]).results[0]["out"]
```

```python
FEATURES = 39
DIM = 64
HID = 128
BATCH = 512
BLOCK = 128
BLOCKS = BATCH // BLOCK
HALF = BLOCK // 2
SUB = HALF // 2
WINDOW = 32
GROUP = 8
PAIRS = 400
TOP1 = 512
TOP2 = 256

HALVES = (
    {"X": (0, 7), "M": (7, 6), "Y": (13, 7)},
    {"X": (20, 7), "M": (27, 5), "Y": (32, 7)},
)
FIRST = (0, 20)
COUNT = (20, 19)
SEGMENTS = ("MM", "XX", "XY", "YY", "MX", "MY")


def tri(n, i):
    return i * n - i * (i - 1) // 2


def layout_of_half(half):
    at, start = 0, {}
    for name in SEGMENTS:
        start[name] = at
        n, m = (HALVES[half][g][1] for g in name)
        at += n * (n + 1) // 2 if name[0] == name[1] else n * m
    return start, at


START = [layout_of_half(half)[0] for half in (0, 1)]
ROWS = [layout_of_half(half)[1] for half in (0, 1)]
PAIR_BASE = (0, ROWS[0])

CHUNKS = (
    dict(half=0, lo=0, hi=START[0]["MX"], window=20, own=(0, 0)),
    dict(half=0, lo=START[0]["YY"], hi=ROWS[0], window=7, own=(27, 12)),
    dict(half=1, lo=0, hi=START[1]["MX"], window=0, own=(20, 7)),
    dict(half=1, lo=START[1]["YY"], hi=ROWS[1], window=27, own=(0, 27)),
)
PAIR_ROWS = [c["hi"] - c["lo"] for c in CHUNKS]
CHUNK_ROWS = [c["hi"] - c["lo"] + c["own"][1] for c in CHUNKS]
WRAPPED = 59

MOMENT_TILES = tuple(
    [(3, PAIR_ROWS[3] + 4 * t, 4, 0, 32) for t in range(6)]
    + [(3, PAIR_ROWS[3] + 24, 3, 0, 32)]
    + [(1, PAIR_ROWS[1] + 6 * t, 6, 20, 12) for t in range(2)]
    + [(2, PAIR_ROWS[2], 7, 20, 7)]
)
TILES = len(MOMENT_TILES)


def slot_of(chunk, feature):
    slot = (feature - CHUNKS[chunk]["window"]) % FEATURES
    return slot if slot < WINDOW else None


def group_of(feature):
    half = int(feature >= FIRST[1])
    for name, (first, count) in HALVES[half].items():
        if first <= feature < first + count:
            return half, name, feature - first


def pair_features(half):
    out = []
    for name in SEGMENTS:
        (f, n), (g, m) = (HALVES[half][x] for x in name)
        if name[0] == name[1]:
            out += [(f + i, f + j) for i in range(n) for j in range(i, n)]
        else:
            out += [(f + i, g + j) for i in range(n) for j in range(m)]
    return out


def pieces_of_chunk(chunk):
    c = CHUNKS[chunk]
    out = []
    for name in SEGMENTS:
        row = START[c["half"]][name] - c["lo"]
        if not 0 <= row < PAIR_ROWS[chunk]:
            continue
        (f, n), (g, m) = (HALVES[c["half"]][x] for x in name)
        if name[0] == name[1]:
            out += [(row + tri(n, i), f + i, 1, f + i, n - i) for i in range(n)]
        else:
            out.append((row, f, n, g, m))
    return out


def rows_with(half, name, other):
    group, place = name
    n = HALVES[half][other][1]
    if group == other:
        base = START[half][group * 2]
        out = [(base + tri(n, place), 1, place, n - place)]
        out += [(base + tri(n, j) + place - j, 1, j, 1) for j in range(place)]
    elif group + other in START[half]:
        out = [(START[half][group + other] + place * n, 1, 0, n)]
    else:
        step = HALVES[half][group][1]
        out = [(START[half][other + group] + place, step, 0, n)]
    found = []
    for row, step, first, count in out:
        chunk = 2 * half + int(row >= START[half]["MX"])
        found.append((chunk, row - CHUNKS[chunk]["lo"], step, first, count))
    return found


CROSS = COUNT[0] * COUNT[1]


def extra_of(i):
    half, group, _ = group_of(i)
    if group == "Y":
        return 0, START[half]["YY"]
    if group == "X":
        return START[half]["MX"], ROWS[half] - START[half]["MX"]
    return None


def additions_of(i):
    half, group, place = group_of(i)
    other = 1 - half
    out = []
    for g, (first, _) in HALVES[half].items():
        for chunk, row, step, at, count in rows_with(half, (group, place), g):
            a = first + at - FIRST[half]
            if half == 0:
                source, steps = a * COUNT[1], (COUNT[1], 1)
            else:
                source, steps = a, (1, COUNT[1])
            out.append((source, [(steps[0], count), (steps[1], COUNT[other])],
                        chunk, slot_of(chunk, FIRST[other]), row, [(0, step), (1, 0)]))
    x, m, y = (HALVES[half][g] for g in "XMY")
    start = START[half]
    one, two = 2 * half, 2 * half + 1
    if group == "Y":
        for j in range(m[1]):
            out.append((CROSS + start["MM"] + tri(m[1], j), [(1, m[1] - j)],
                        two, slot_of(two, m[0] + j), start["MY"] - CHUNKS[two]["lo"] + j * y[1] + place, [(1, 0)]))
        for j in range(x[1]):
            out.append((CROSS + start["XX"] + tri(x[1], j), [(1, x[1] - j)],
                        one, slot_of(one, x[0] + j), start["XY"] + j * y[1] + place, [(1, 0)]))
        for chunk, row, step, at, count in rows_with(half, ("Y", place), "Y"):
            out.append((CROSS + start["XY"] + at, [(y[1], x[1]), (1, count)],
                        chunk, slot_of(chunk, x[0]), row, [(1, 0), (0, step)]))
    if group == "X":
        extra = CROSS - start["MX"]
        for chunk, row, step, at, count in rows_with(half, ("X", place), "X"):
            out.append((extra + start["MX"] + at, [(x[1], m[1]), (1, count)],
                        chunk, slot_of(chunk, m[0]), row, [(1, 0), (0, step)]))
        out.append((extra + start["MY"], [(y[1], m[1]), (1, y[1])],
                    one, slot_of(one, m[0]), start["XY"] + place * y[1], [(1, 0), (0, 1)]))
    return out


def build(nc, args):
    import concourse.bass as bass
    from concourse import mybir
    from contextlib import ExitStack

    FP = mybir.dt.float32
    ALU = mybir.AluOpType
    ACT = mybir.ActivationFunctionType

    ctx = ExitStack()
    with ctx:
        def sb(name, shape, dt=FP):
            return ctx.enter_context(nc.sbuf_tensor(name, shape, dt))

        def sem(name):
            return ctx.enter_context(nc.semaphore(name))

        SLOTS = len(CHUNKS) * WINDOW
        shared = sb("shared", [128, SLOTS * 128])
        weights_h = shared[:, :].rearrange("h (s r) -> h s r", r=128)
        products = [shared[:, n * 4096:(n + 1) * 4096].rearrange("p (b r) -> p b r", r=128) for n in range(2)]
        moments = [shared[:, (2 + n) * 4096:(3 + n) * 4096].rearrange("r (c q) -> r c q", c=WINDOW) for n in range(2)]
        weights = sb("weights", [128, SLOTS, 128])
        pair_w = [weights[:, 8 * n:8 * n + 7, :] for n in range(2)]
        pair_sum = weights[:, 16:23, :]
        w1 = sb("w1", [128, FEATURES * 128])
        z1_w = w1[:, 0:TILES * 128].rearrange("p (t h) -> p t h", h=128)
        second = w1[:, TILES * 128:2 * TILES * 128].rearrange("p (t s) -> p t s", s=128)
        z = w1[:, 2 * TILES * 128:2 * TILES * 128 + 2 * BATCH]
        rows_in = sb("rows_in", [128, (FEATURES + 2) * DIM])
        xt_all = sb("xt", [128, 2 * FEATURES * HALF])
        xt = [xt_all[:, n * FEATURES * HALF:(n + 1) * FEATURES * HALF].rearrange("p (f b) -> p f b", b=HALF) for n in (0, 1)]
        pair_t = xt_all[:, FEATURES * HALF:FEATURES * HALF + PAIRS + CROSS]
        z1_sum = xt_all[:, FEATURES * HALF + PAIRS + CROSS:][:, 0:TILES * 128].rearrange("p (t h) -> p t h", h=128)
        z1_part = weights[:, 24:24 + TILES, :]
        xd = sb("xd", [128, HALF, 2, WRAPPED])
        ids_now = sb("ids_now", [128, FEATURES], mybir.dt.int32)
        gate = sb("gate", [128, 2])
        ident = sb("ident", [128, 128])
        top1_w = rows_in[:, 0:2 * TOP1].rearrange("p (t n) -> p t n", n=TOP1)
        top1_wd = rows_in[0:16, 2 * TOP1:2 * TOP1 + TOP1]
        top2_w = rows_in[:, 3 * TOP1:3 * TOP1 + 4 * TOP2].rearrange("p (t n) -> p t n", n=TOP2)
        hidden1 = xt_all[:, 0:4 * BATCH].rearrange("p (t s) -> p t s", s=BATCH)
        xd_flat = xd[:, :, :, :].rearrange("p b q f -> p (b q f)")
        hidden2 = xd_flat[:, 0:2 * BATCH].rearrange("p (t s) -> p t s", s=BATCH)
        dense = xd_flat[0:16, 2 * BATCH:3 * BATCH]
        answer = xd_flat[0:1, 3 * BATCH:4 * BATCH]
        columns = xd_flat[:, 4 * BATCH:4 * BATCH + 8]
        bank = [ctx.enter_context(nc.psum_tensor(f"bank{n}", [128, 512], FP)) for n in range(8)]
        ring, flip, z2_bank, z1_bank = bank[0:4], bank[4:6], bank[6], bank[7]

        w0_loaded = sem("w0_loaded")
        w1_loaded = [sem(f"w1_loaded{n}") for n in range(4)]
        ids_loaded = sem("ids_loaded")
        z1w_loaded = sem("z1w_loaded")
        z1w_moved = sem("z1w_moved")
        top_loaded = sem("top_loaded")
        second_loaded = [sem(f"second_loaded{c}") for c in range(4)]
        answer_stored = sem("answer_stored")
        ident_set = sem("ident_set")
        gate_passed = sem("gate_passed")
        edges_zeroed = sem("edges_zeroed")
        xd_zeroed = sem("xd_zeroed")
        places_zeroed = sem("places_zeroed")
        gathered = sem("gathered")
        pairs_summed = sem("pairs_summed")
        pairs_flipped = sem("pairs_flipped")
        pairs_ready = sem("pairs_ready")
        direct_a = sem("direct_a")
        direct_b = sem("direct_b")
        placed_a = [sem("placed_a_even"), sem("placed_a_odd")]
        placed_b = sem("placed_b")
        extra_done = sem("extra_done")
        added = sem("added")
        turned = sem("turned")
        kept = sem("kept")
        flipped = sem("flipped")
        flip_freed = sem("flip_freed")
        xd_ready = sem("xd_ready")
        products_ready = sem("products_ready")
        moments_out = sem("moments_out")
        moments_ready = sem("moments_ready")
        moments_freed = sem("moments_freed")
        z1w_ready = sem("z1w_ready")
        z1_done = sem("z1_done")
        z_kept = sem("z_kept")
        top_done = sem("top_done")
        top_kept = sem("top_kept")

        CHUNK_TILES = [sum(t[0] == chunk for t in MOMENT_TILES) for chunk in range(4)]
        C_BANKS = SLOTS // 4
        HALF_BANKS = C_BANKS // 2
        EVEN, ODD = (FEATURES + 1) // 2, FEATURES // 2
        W1_PIECE = -(-FEATURES // len(w1_loaded))
        TURN_AT = FEATURES - HALF_BANKS
        FLIP_AT = TURN_AT + 1
        FLIP_BANKS = 10
        GROUPS = HALF // GROUP
        SUB_GROUPS = GROUPS // 2
        BLOCK_GROUPS = len(CHUNKS) * GROUPS
        RING = len(ring)
        FREE_GROUPS = 2 * SUB_GROUPS

        def place_direct(op, tail, i, half, done):
            source = bank[4 * half + i % 4]
            moves = []
            one, two = 2 * half, 2 * half + 1
            if slot_of(one, i) is not None:
                moves.append((one, 0, START[half]["MX"]))
            if slot_of(two, i) is not None:
                own_y = group_of(i)[:2] == (half, "Y")
                moves.append((two, START[half]["YY" if own_y else "MX"], ROWS[half]))
            for n, (chunk, lo, hi) in enumerate(moves):
                row = lo - CHUNKS[chunk]["lo"]
                ins = op(weights_h[:, WINDOW * chunk + slot_of(chunk, i), row:row + hi - lo],
                         source[:, lo:hi], *tail)
                if n == len(moves) - 1:
                    ins.then_inc(done, 1)

        def ap_of(base, offset, axes):
            return bass.AP(base.tensor, base.offset + offset, [list(base.ap[0])] + [list(a) for a in axes])

        block = ctx.enter_context(nc.Block())

        @block.sync
        def _(sp):
            sp.dma_start(pair_w[0], args["pairs_a"].rearrange("(t p) h -> p t h", p=128)).then_inc(w0_loaded, 16)
            sp.dma_start(pair_w[1], args["pairs_b"].rearrange("(t p) h -> p t h", p=128)).then_inc(w0_loaded, 16)
            for n, loaded in enumerate(w1_loaded):
                cols = slice(128 * W1_PIECE * n, min(128 * W1_PIECE * (n + 1), 128 * FEATURES))
                sp.dma_start(w1[:, cols], args["w1"][:, cols]).then_inc(loaded, 16)
            sp.dma_start(z1_sum, args["z1_a"].rearrange("t p h -> p t h")).then_inc(z1w_loaded, 16)
            sp.dma_start(z1_part, args["z1_b"].rearrange("t p h -> p t h")).then_inc(z1w_loaded, 16)
            sp.wait_ge(z1w_ready, 1)
            sp.wait_ge(extra_done, FEATURES)
            sp.dma_start(z1_w, z1_sum).then_inc(z1w_moved, 16)
            with sp.Fori(0, BLOCKS) as k:
                sp.wait_ge(z_kept, 2 * (k + 1))
                for chunk in (1, 2, 3):
                    sp.wait_ge(moments_ready, RING + BLOCK_GROUPS * k + GROUPS * (chunk + 1))
                    for t, (of, row, n, slot, slots) in enumerate(MOMENT_TILES):
                        if of == chunk:
                            src = moments[chunk % 2][row:row + n, slot:slot + slots, :]
                            sp.dma_start(second[0:n * slots, t, :], src).then_inc(second_loaded[chunk], 16)
            sp.wait_ge(flipped, 1 + FLIP_BANKS * BLOCKS)
            sp.dma_start(top1_w, args["W_top1"][0:256, :].rearrange("(t p) n -> p t n", p=128)).then_inc(top_loaded, 16)
            sp.dma_start(top1_wd, args["W_top1"][256:272, :]).then_inc(top_loaded, 16)
            sp.dma_start(top2_w, args["W_top2"].rearrange("(t p) n -> p t n", p=128)).then_inc(top_loaded, 16)
            sp.wait_ge(moments_out, FREE_GROUPS + BLOCK_GROUPS * BLOCKS)
            sp.dma_start(dense, args["dense_t"]).then_inc(top_loaded, 16)
            sp.dma_start(columns, args["columns"]).then_inc(top_loaded, 16)
            sp.wait_ge(top_kept, 7)
            sp.dma_start(args["out"].rearrange("s o -> o s"), answer).then_inc(answer_stored, 16)
            sp.wait_ge(answer_stored, 16)

        @block.gpsimd
        def _(pool):
            pool.memset(rows_in[:, 0:DIM], 0.0).then_inc(edges_zeroed, 1)
            pool.memset(rows_in[:, (FEATURES + 1) * DIM:], 0.0).then_inc(flipped, 1)
            pool.memset(gate[:, :], 0.0).then_inc(gate_passed, 1)
            pool.memset(ident[:, :], 1.0).then_inc(ident_set, 1)
            pool.wait_ge(ident_set, 1)
            pool.affine_select(out=ident[:, :], in_=ident[:, :], compare_op=ALU.is_equal, fill=0.0,
                               base=0, pattern=[[-1, 128]], channel_multiplier=1).then_inc(ident_set, 1)
            pool.memset(xd[:, :, :, :].rearrange("p b q f -> p (b q f)"), 0.0).then_inc(xd_zeroed, 1)
            with pool.Fori(0, BLOCKS) as k:
                pool.wait_ge(gate_passed, k + 1)
                pool.wait_ge(flipped, 1 + FLIP_BANKS * k)
                pool.dma_start(ids_now[:, :], args["ids"][bass.ts(k, BLOCK), :]).then_inc(ids_loaded, 16)
                pool.wait_ge(ids_loaded, 16 * (k + 1))
                pool.tensor_tensor(gate[:, 1:2], gate[:, 0:1], gate[:, 0:1], ALU.add).then_inc(gate_passed, 1)
                for f in range(FEATURES):
                    pool.indirect_dma_start(
                        rows_in[:, (f + 1) * DIM:(f + 2) * DIM], None, args[f"tbl_{f}"],
                        bass.IndirectOffsetOnAxis(ap=ids_now[:, f:f + 1], axis=0)).then_inc(gathered, 16)

        @block.scalar
        def _(act):
            for n, width in enumerate((512, PAIRS + CROSS - 512)):
                act.wait_ge(pairs_flipped, n + 1)
                act.activation(pair_t[:, 512 * n:512 * n + width], ring[n][:, 0:width], ACT.Copy).then_inc(pairs_ready, 1)
            act.wait_ge(places_zeroed, 1)
            for i in range(0, FEATURES, 2):
                act.wait_ge(direct_a, i + 1)
                place_direct(act.activation, (ACT.Copy,), i, 0, placed_a[0])
            for i in range(FEATURES):
                act.wait_ge(direct_b, i + 1)
                place_direct(act.activation, (ACT.Copy,), i, 1, placed_b)

            def flip_out(k, j):
                at = FEATURES * HALF * (k % 2)
                act.wait_ge(flipped, 1 + FLIP_BANKS * k + j + 1)
                tiles = flip[j % 2][:, :].rearrange("p (t s) -> p t s", s=BLOCK)
                low, high = int(j == 0), 3 if j == FLIP_BANKS - 1 else 4
                for part, lo, hi, f, of in ((0, low, 4, 4 * j - 1 + low, 0), (64, 0, high, 4 * j, HALF)):
                    out = xt_all[part:part + 64, bass.ds(at + HALF * f, HALF * (hi - lo))]
                    last = act.activation(out.rearrange("p (t s) -> p t s", s=HALF),
                                          tiles[part:part + 64, lo:hi, of:of + HALF], ACT.Copy)
                last.then_inc(flip_freed, 1)

            def spread(k):
                at = FEATURES * HALF * (k % 2)
                act.wait_ge(flip_freed, FLIP_BANKS * (k + 1))
                for f, to, n in ((20, 20, 19), (0, 39, 13), (0, 0, 20), (13, 52, 7)):
                    for q in range(2):
                        part = slice(64 * q, 64 * q + 64)
                        rows = xt_all[part, bass.ds(at + HALF * f, HALF * n)].rearrange("p (f b) -> p b f", b=HALF)
                        last = act.activation(xd[part, :, q, to:to + n], rows, ACT.Copy)
                    last.then_inc(xd_ready, 1)

            def keep(v, source):
                act.wait_ge(turned, v + 1)
                act.activation(weights[:, 4 * v:4 * v + 4, :].rearrange("r s h -> r (s h)"),
                               source[:, :], ACT.Copy).then_inc(kept, 1)

            act.wait_ge(z1w_ready, 1)
            for i in range(TURN_AT, FEATURES):
                keep(i - TURN_AT, bank[6 + (i - TURN_AT) % 2])
                if 0 <= i - FLIP_AT < FLIP_BANKS:
                    flip_out(0, i - FLIP_AT)
            act.wait_ge(xd_zeroed, 1)
            spread(0)
            for v in range(HALF_BANKS, C_BANKS):
                keep(v, bank[4 + v % 4])

            def chunk_out(k, chunk):
                act.wait_ge(moments_freed, 4 * k + chunk + 1)
                if chunk == 3:
                    act.wait_ge(second_loaded[1], 16 * CHUNK_TILES[1] * (k + 1))
                n = CHUNK_ROWS[chunk]
                out = moments[chunk % 2].rearrange("r c (q b) -> r c q b", q=2)
                for g in range(GROUPS):
                    act.wait_ge(moments_out, FREE_GROUPS + BLOCK_GROUPS * k + GROUPS * chunk + g + 1)
                    act.activation(out[0:n, :, :, GROUP * g:GROUP * (g + 1)],
                                   ring[g % 4][0:n, :].rearrange("r (b q c) -> r c q b", b=GROUP, q=2),
                                   ACT.Copy).then_inc(moments_ready, 1)

            def block_out(k, last):
                chunk_out(k, 1)
                chunk_out(k, 2)
                if not last:
                    act.wait_ge(products_ready, 8 * k + 1)
                    for j in range(FLIP_BANKS):
                        flip_out(k + 1, j)
                chunk_out(k, 3)
                if not last:
                    act.wait_ge(moments_out, FREE_GROUPS + BLOCK_GROUPS * (k + 1))
                    spread(k + 1)
                    act.wait_ge(second_loaded[2], 16 * CHUNK_TILES[2] * (k + 1))
                    chunk_out(k + 1, 0)
                act.wait_ge(moments_freed, 2 + 4 * (k + 1))
                act.activation(z[:, bass.ds(BATCH + BLOCK * k, BLOCK)], z2_bank[:, 0:BLOCK], ACT.Copy).then_inc(z_kept, 1)
                act.wait_ge(z1_done, k + 1)
                act.activation(z[:, bass.ds(BLOCK * k, BLOCK)], z1_bank[:, 0:BLOCK], ACT.Copy).then_inc(z_kept, 1)

            chunk_out(0, 0)
            with act.Fori(0, BLOCKS - 1) as k:
                block_out(k, False)
            block_out(BLOCKS - 1, True)
            act.wait_ge(top_loaded, 80)
            for t in range(4):
                act.wait_ge(top_done, t + 1)
                act.activation(hidden1[:, t, :], ring[t][:, :], ACT.Relu, bias=columns[:, t:t + 1]).then_inc(top_kept, 1)
            for t in range(2):
                act.wait_ge(top_done, t + 5)
                act.activation(hidden2[:, t, :], flip[t][:, :], ACT.Relu, bias=columns[:, 4 + t:5 + t]).then_inc(top_kept, 1)
            act.wait_ge(top_done, 7)
            act.activation(answer, z1_bank[0:1, :], ACT.Copy).then_inc(top_kept, 1)

        @block.vector
        def _(dve):
            for chunk in range(4):
                nc.vector.memset(weights_h[:, WINDOW * chunk:WINDOW * (chunk + 1), PAIR_ROWS[chunk]:], 0.0)
            for half in (0, 1):
                two = 2 * half + 1
                first = slot_of(two, HALVES[half]["Y"][0])
                yy = START[half]["MX"] - START[half]["YY"]
                for lo, hi in ((0, first), (first + 7, WINDOW)):
                    if hi > lo:
                        last = nc.vector.memset(weights_h[:, WINDOW * two + lo:WINDOW * two + hi, 0:yy], 0.0)
            last.then_inc(places_zeroed, 1)
            dve.wait_ge(w0_loaded, 32)
            nc.vector.tensor_tensor(pair_sum, pair_w[0], pair_w[1], ALU.add).then_inc(pairs_summed, 1)
            for i in range(1, FEATURES, 2):
                dve.wait_ge(direct_a, i + 1)
                place_direct(nc.vector.tensor_copy, (), i, 0, placed_a[1])
            dve.wait_ge(z1w_loaded, 32)
            nc.vector.tensor_tensor(z1_sum, z1_sum, z1_part, ALU.add).then_inc(z1w_ready, 1)
            for i in range(FEATURES):
                dve.wait_ge(extra_done, i + 1)
                if i:
                    dve.wait_ge(added, i)
                if i == 0:
                    dve.wait_ge(placed_a[0], EVEN)
                    dve.wait_ge(placed_a[1], ODD)
                if i == FIRST[1]:
                    dve.wait_ge(placed_b, FEATURES)
                moves = additions_of(i)
                for n, (col, axes, chunk, slot, row, steps) in enumerate(moves):
                    source = ap_of(ring[i % 4][:, :], col, axes)
                    place = ap_of(shared[:, :], (WINDOW * chunk + slot) * 128 + row,
                                  [(128 * s + r, count) for (s, r), (_, count) in zip(steps, axes)])
                    ins = nc.vector.tensor_tensor(place, source, place, ALU.add)
                ins.then_inc(added, 1)

            def multiply(k, x):
                dve.wait_ge(flip_freed, FLIP_BANKS * (k + 1))
                for chunk in range(4):
                    for s in range(2):
                        dve.wait_ge(moments_out, SUB_GROUPS * (8 * k + 2 * chunk + s + 1))
                        b = slice(SUB * s, SUB * (s + 1))
                        own, count = CHUNKS[chunk]["own"]
                        if count:
                            row = PAIR_ROWS[chunk]
                            nc.vector.tensor_copy(products[s][:, :, row:row + count],
                                                  x[:, own:own + count, b].rearrange("p f b -> p b f"))
                        for row, fa, na, fb, nb in pieces_of_chunk(chunk):
                            out = products[s][:, :, row:row + na * nb].rearrange("p b (i j) -> p b i j", i=na)
                            one, two = x[:, fa:fa + na, b], x[:, fb:fb + nb, b]
                            one = one.rearrange("p (f o) b -> p b f o", o=1).to_broadcast([128, SUB, na, nb])
                            two = two.rearrange("p (o f) b -> p b o f", o=1).to_broadcast([128, SUB, na, nb])
                            last = nc.vector.tensor_tensor(out, one, two, ALU.mult)
                        last.then_inc(products_ready, 1)

            with dve.Fori(0, BLOCKS // 2) as two_blocks:
                multiply(2 * two_blocks, xt[0])
                multiply(2 * two_blocks + 1, xt[1])

        @block.tensor
        def _(pe):
            pe.wait_ge(ident_set, 2)
            pe.wait_ge(pairs_summed, 1)
            for t in range(7):
                n = min(128, PAIRS + CROSS - 128 * t)
                last = nc.tensor.transpose(ring[t // 4][:, 128 * (t % 4):128 * (t % 4) + n],
                                           pair_sum[0:n, t, :], ident[0:n, 0:n])
                if t in (3, 6):
                    last.then_inc(pairs_flipped, 1)
            pe.wait_ge(pairs_ready, 2)

            def direct(i, half, done):
                col = PAIR_BASE[half]
                nc.tensor.matmul(bank[4 * half + i % 4][:, 0:ROWS[half]], w1[:, 128 * i:128 * (i + 1)],
                                 pair_t[:, col:col + ROWS[half]], start=True, stop=True).then_inc(done, 1)

            for i in range(FEATURES):
                if i % W1_PIECE == 0:
                    pe.wait_ge(w1_loaded[i // W1_PIECE], 16)
                if i >= 4:
                    pe.wait_ge(placed_a[i % 2], i // 2 - 1)
                direct(i, 0, direct_a)

            def flip_bank(k, j):
                if j == 0:
                    pe.wait_ge(gathered, 16 * FEATURES * (k + 1))
                for t in range(4 * j, 4 * j + 4):
                    last = nc.tensor.transpose(flip[j % 2][:, BLOCK * (t % 4):BLOCK * (t % 4 + 1)],
                                               rows_in[:, DIM * t:DIM * (t + 2)], ident[:, :])
                return last

            def turn(v, out):
                for s in range(4):
                    last = nc.tensor.transpose(out[:, 128 * s:128 * (s + 1)], weights_h[:, 4 * v + s, :], ident[:, :])
                last.then_inc(turned, 1)

            pe.wait_ge(placed_a[0], EVEN)
            pe.wait_ge(placed_a[1], ODD)
            for i in range(FEATURES):
                if i >= 4:
                    pe.wait_ge(added, i - 3)
                extra = extra_of(i)
                w = w1[:, 128 * i:128 * (i + 1)]
                last = nc.tensor.matmul(ring[i % 4][:, 0:CROSS], w, pair_t[:, PAIRS:], start=True, stop=True)
                if extra:
                    col = PAIR_BASE[group_of(i)[0]] + extra[0]
                    last = nc.tensor.matmul(ring[i % 4][:, CROSS:CROSS + extra[1]], w, pair_t[:, col:col + extra[1]],
                                            start=True, stop=True)
                last.then_inc(extra_done, 1)
                for j in range(2 * i, min(2 * i + 2, FEATURES)):
                    if j >= 4:
                        pe.wait_ge(placed_b, j - 3)
                    direct(j, 1, direct_b)
                if i >= TURN_AT:
                    v = i - TURN_AT
                    if v == 0:
                        pe.wait_ge(added, FIRST[1])
                        pe.wait_ge(placed_b, FEATURES)
                    if v >= 2:
                        pe.wait_ge(kept, v - 1)
                    turn(v, bank[6 + v % 2])
                if 0 <= i - FLIP_AT < FLIP_BANKS:
                    j = i - FLIP_AT
                    if j == 0:
                        pe.wait_ge(edges_zeroed, 1)
                    if j >= 2:
                        pe.wait_ge(flip_freed, j - 1)
                    flip_bank(0, j).then_inc(flipped, 1)
            pe.wait_ge(flip_freed, FLIP_BANKS)
            nc.tensor.matmul(flip[0][0:1, 0:1], ident[:, 0:1], ident[:, 0:1], start=True, stop=True).then_inc(moments_out, FREE_GROUPS)
            pe.wait_ge(added, FEATURES)
            for v in range(HALF_BANKS, C_BANKS):
                if v >= HALF_BANKS + 2:
                    pe.wait_ge(kept, max(v - 3, HALF_BANKS))
                turn(v, bank[4 + v % 4])
            nc.tensor.matmul(ring[0][0:1, 0:1], ident[:, 0:1], ident[:, 0:1], start=True, stop=True).then_inc(moments_freed, 2)
            pe.wait_ge(kept, C_BANKS)
            nc.tensor.matmul(ring[0][0:1, 0:1], ident[:, 0:1], ident[:, 0:1], start=True, stop=True).then_inc(moments_ready, RING)
            nc.tensor.matmul(z1_bank[0:1, 0:1], ident[:, 0:1], ident[:, 0:1], start=True, stop=True).then_inc(z_kept, 2)
            pe.wait_ge(z1w_moved, 16)

            def take_moments(k, chunk):
                n, window = CHUNK_ROWS[chunk], CHUNKS[chunk]["window"]
                for g in range(GROUPS):
                    s, q = divmod(g, SUB_GROUPS)
                    if q == 0:
                        pe.wait_ge(products_ready, 8 * k + 2 * chunk + s + 1)
                    pe.wait_ge(moments_ready, BLOCK_GROUPS * k + GROUPS * chunk + g + 1)
                    for j in range(GROUP):
                        for lo, hi in ((0, 64), (64, n)):
                            out = ring[g % 4][lo:hi, 64 * j:64 * (j + 1)].rearrange("r (q c) -> r q c", q=2)
                            last = nc.tensor.matmul(out, products[s][:, GROUP * q + j, lo:hi],
                                                    xd[:, GROUP * g + j, :, window:window + WINDOW], start=True, stop=True)
                    last.then_inc(moments_out, 1)

            def weigh(k, chunk, flips):
                n = CHUNK_ROWS[chunk]
                pe.wait_ge(moments_ready, RING + BLOCK_GROUPS * k + GROUPS * (chunk + 1))
                if chunk == 0:
                    pe.wait_ge(z_kept, 2 * (k + 1))
                for c in range(WINDOW):
                    last = nc.tensor.matmul(z2_bank[:, 0:BLOCK], weights[0:n, WINDOW * chunk + c, :],
                                            moments[chunk % 2][0:n, c, :],
                                            start=(chunk == 0 and c == 0), stop=(chunk == 3 and c == WINDOW - 1))
                    if flips and c % 3 == 1 and c // 3 < FLIP_BANKS:
                        j = c // 3
                        pe.wait_ge(flip_freed, FLIP_BANKS * (k + 1) + j - 1)
                        flip_bank(k + 1, j).then_inc(flipped, 1)
                last.then_inc(moments_freed, 1)

            def whole_block(k, last_one):
                pe.wait_ge(xd_ready, 4 * (k + 1))
                take_moments(k, 1)
                weigh(k, 0, False)
                take_moments(k, 2)
                weigh(k, 1, not last_one)
                take_moments(k, 3)
                weigh(k, 2, False)
                if not last_one:
                    pe.wait_ge(xd_ready, 4 * (k + 1) + 2)
                    take_moments(k + 1, 0)
                weigh(k, 3, False)
                for chunk in (1, 2, 3):
                    pe.wait_ge(second_loaded[chunk], 16 * CHUNK_TILES[chunk] * (k + 1))
                for t, (_, _, n, _, slots) in enumerate(MOMENT_TILES):
                    last = nc.tensor.matmul(z1_bank[:, 0:BLOCK], z1_w[0:n * slots, t, :], second[0:n * slots, t, :],
                                            start=(t == 0), stop=(t == TILES - 1))
                last.then_inc(z1_done, 1)

            pe.wait_ge(xd_ready, 2)
            take_moments(0, 0)
            with pe.Fori(0, BLOCKS - 1) as k:
                whole_block(k, False)
            whole_block(BLOCKS - 1, True)
            pe.wait_ge(top_loaded, 80)
            pe.wait_ge(z_kept, 2 + 2 * BLOCKS)
            for t in range(4):
                cols = slice(128 * t, 128 * (t + 1))
                nc.tensor.matmul(ring[t][:, :], top1_w[:, 0, cols], z[:, 0:BATCH], start=True, stop=False)
                nc.tensor.matmul(ring[t][:, :], top1_w[:, 1, cols], z[:, BATCH:2 * BATCH], start=False, stop=False)
                nc.tensor.matmul(ring[t][:, :], top1_wd[:, cols], dense, start=False, stop=True).then_inc(top_done, 1)
            pe.wait_ge(top_kept, 4)
            for t in range(2):
                for s in range(4):
                    last = nc.tensor.matmul(flip[t][:, :], top2_w[:, s, 128 * t:128 * (t + 1)], hidden1[:, s, :],
                                            start=(s == 0), stop=(s == 3))
                last.then_inc(top_done, 1)
            pe.wait_ge(top_kept, 6)
            for s in range(2):
                last = nc.tensor.matmul(z1_bank[0:1, :], columns[:, 6 + s:7 + s], hidden2[:, s, :], start=(s == 0), stop=(s == 1))
            last.then_inc(top_done, 1)


def pair_index():
    zero = FEATURES * FEATURES
    pairs = pair_features(0) + pair_features(1)
    pairs += [(a, b) for a in range(COUNT[0]) for b in range(FIRST[1], FEATURES)]
    one = [a * FEATURES + b for a, b in pairs]
    two = [b * FEATURES + a if a != b else zero for a, b in pairs]
    fill = [zero] * (-len(pairs) % 128)
    return one + fill, two + fill


def moment_index():
    zero = FEATURES * FEATURES
    one, two = [], []
    for chunk, row, n, slot, slots in MOMENT_TILES:
        rows_one, rows_two = [], []
        for r in range(row, row + n):
            x = CHUNKS[chunk]["own"][0] + r - PAIR_ROWS[chunk]
            for s in range(slot, slot + slots):
                f = (CHUNKS[chunk]["window"] + s) % FEATURES
                rows_one.append(x * FEATURES + f)
                both = chunk == 3 and not (x < FIRST[1] and f < FIRST[1])
                rows_two.append(f * FEATURES + x if both else zero)
        fill = [zero] * (128 - n * slots)
        one += rows_one + fill
        two += rows_two + fill
    return one, two


def kernel(**inputs):
    import numpy as np
    import concourse.bacc as bacc
    from concourse import mybir
    from concourse.bass_utils import run_bass_kernel_spmd as run

    nc = bacc.Bacc("TRN2", target_bir_lowering=False, num_devices=1)
    w0 = np.asarray(inputs["L0_rec_W0"]).reshape(FEATURES * FEATURES, HID)
    w0 = np.concatenate([w0, np.zeros((1, HID), w0.dtype)])
    pairs_a, pairs_b = pair_index()
    z1_a, z1_b = moment_index()
    arrays = {
        "ids": inputs["ids"],
        "pairs_a": w0[np.array(pairs_a)],
        "pairs_b": w0[np.array(pairs_b)],
        "z1_a": w0[np.array(z1_a)].reshape(TILES, 128, HID),
        "z1_b": w0[np.array(z1_b)].reshape(TILES, 128, HID),
        "w1": np.asarray(inputs["L0_rec_W1"]).transpose(1, 0, 2).reshape(HID, FEATURES * HID),
        "dense_t": np.asarray(inputs["dense_ctx"]).T,
        "W_top1": inputs["W_top1"],
        "W_top2": inputs["W_top2"],
        "columns": np.concatenate([np.asarray(inputs[n]).reshape(-1, 128) for n in ("b_top1", "b_top2", "W_top3")]).T,
    }
    arrays.update({f"tbl_{f}": inputs[f"tbl_{f}"] for f in range(FEATURES)})
    arrays = {f"in_{n}": np.ascontiguousarray(a) for n, a in arrays.items()}
    args = {n[3:]: nc.dram_tensor(n, a.shape, mybir.dt.from_np(a.dtype), kind="ExternalInput").ap()
            for n, a in arrays.items()}
    args["out"] = nc.dram_tensor("out", (BATCH, 1), mybir.dt.float32, kind="ExternalOutput").ap()
    build(nc, args)
    return run(nc, [arrays], core_ids=[0]).results[0]["out"]
```

```python
FEATURES = 39
DIM = 64
HID = 128
BATCH = 512
BLOCK = 128
BLOCKS = BATCH // BLOCK
HALF = BLOCK // 2
SUB = HALF // 2
WINDOW = 32
GROUP = 8
PAIRS = 400
TOP1 = 512
TOP2 = 256

HALVES = (
    {"X": (0, 7), "M": (7, 6), "Y": (13, 7)},
    {"X": (20, 7), "M": (27, 5), "Y": (32, 7)},
)
FIRST = (0, 20)
COUNT = (20, 19)
SEGMENTS = ("MM", "XX", "XY", "YY", "MX", "MY")




def tri(n, i):
    return i * n - i * (i - 1) // 2


def pairs_within(n):
    if n % 2:
        return [(i, (i + d) % n) for i in range(n) for d in range(n // 2 + 1)]
    return [(i, j) for i in range(n) for j in range(i, n)]


def layout_of_half(half):
    at, start = 0, {}
    for name in SEGMENTS:
        start[name] = at
        n, m = (HALVES[half][g][1] for g in name)
        at += n * (n + 1) // 2 if name[0] == name[1] else n * m
    return start, at


START = [layout_of_half(half)[0] for half in (0, 1)]
ROWS = [layout_of_half(half)[1] for half in (0, 1)]
PAIR_BASE = (0, ROWS[0])

CHUNKS = (
    dict(half=0, lo=0, hi=START[0]["MX"], window=20, own=(0, 0)),
    dict(half=0, lo=START[0]["YY"], hi=ROWS[0], window=7, own=(27, 12)),
    dict(half=1, lo=0, hi=START[1]["MX"], window=0, own=(20, 7)),
    dict(half=1, lo=START[1]["YY"], hi=ROWS[1], window=27, own=(0, 27)),
)
PAIR_ROWS = [c["hi"] - c["lo"] for c in CHUNKS]
CHUNK_ROWS = [c["hi"] - c["lo"] + c["own"][1] for c in CHUNKS]
WRAPPED = 59

MOMENT_TILES = tuple(
    [(3, PAIR_ROWS[3] + 4 * t, 4, 0, 32) for t in range(6)]
    + [(3, PAIR_ROWS[3] + 24, 3, 0, 32)]
    + [(1, PAIR_ROWS[1] + 6 * t, 6, 20, 12) for t in range(2)]
    + [(2, PAIR_ROWS[2], 7, 20, 7)]
)
TILES = len(MOMENT_TILES)


def slot_of(chunk, feature):
    slot = (feature - CHUNKS[chunk]["window"]) % FEATURES
    return slot if slot < WINDOW else None


def group_of(feature):
    half = int(feature >= FIRST[1])
    for name, (first, count) in HALVES[half].items():
        if first <= feature < first + count:
            return half, name, feature - first


def pair_features(half):
    out = []
    for name in SEGMENTS:
        (f, n), (g, m) = (HALVES[half][x] for x in name)
        if name[0] == name[1]:
            out += [(f + i, f + j) for i, j in pairs_within(n)]
        else:
            out += [(f + i, g + j) for i in range(n) for j in range(m)]
    return out


def pieces_of_chunk(chunk):
    c = CHUNKS[chunk]
    out = []
    for name in SEGMENTS:
        row = START[c["half"]][name] - c["lo"]
        if not 0 <= row < PAIR_ROWS[chunk]:
            continue
        (f, n), (g, m) = (HALVES[c["half"]][x] for x in name)
        if name[0] != name[1]:
            out.append((row, f, n, g, m, 0))
        elif n % 2:
            span, whole = n // 2 + 1, n - n // 2
            out.append((row, f, whole, f, span, 1))
            for i in range(whole, n):
                out.append((row + i * span, f + i, 1, f + i, n - i, 0))
                out.append((row + i * span + n - i, f + i, 1, f, span - (n - i), 0))
        else:
            out += [(row + tri(n, i), f + i, 1, f + i, n - i, 0) for i in range(n)]
    return out


def rows_with(half, name, other):
    group, place = name
    n = HALVES[half][other][1]
    if group == other and n % 2:
        base, far = START[half][group * 2], n // 2
        row = base + place * (far + 1)
        out = [(row, 1, place, min(far + 1, n - place))]
        if place + far >= n:
            out.append((row + n - place, 1, 0, place + far + 1 - n))
        if place:
            j = max(place - far, 0)
            out.append((base + j * far + place, far, j, place - j))
        if place < far:
            j = place - far + n
            out.append((base + j * far + place + n, far, j, far - place))
    elif group == other:
        base = START[half][group * 2]
        out = [(base + tri(n, place), 1, place, n - place)]
        out += [(base + tri(n, j) + place - j, 1, j, 1) for j in range(place)]
    elif group + other in START[half]:
        out = [(START[half][group + other] + place * n, 1, 0, n)]
    else:
        step = HALVES[half][group][1]
        out = [(START[half][other + group] + place, step, 0, n)]
    found = []
    for row, step, first, count in out:
        chunk = 2 * half + int(row >= START[half]["MX"])
        found.append((chunk, row - CHUNKS[chunk]["lo"], step, first, count))
    return found


CROSS = COUNT[0] * COUNT[1]

SQUARE_M = (False, True)


def extra_pairs(half):
    x, m, y = (HALVES[half][g] for g in "XMY")
    out = [(x[0] + i, y[0] + j, True) for i in range(x[1]) for j in range(y[1])]
    out += [(x[0] + i, x[0] + j, False) for i in range(x[1]) for j in range(x[1])]
    if SQUARE_M[half]:
        return out + [(m[0] + i, m[0] + j, False) for i in range(m[1]) for j in range(m[1])]
    return out + [(m[0] + i, m[0] + j, True) for i in range(m[1]) for j in range(i, m[1])]


EXTRA = [len(extra_pairs(half)) for half in (0, 1)]
EXTRA_BASE = (PAIRS + CROSS, PAIRS + CROSS + EXTRA[0])
PAIR_COLS = PAIRS + CROSS + sum(EXTRA)
PAIR_TILES = -(-PAIR_COLS // 128)


def extra_of(i):
    half, group, _ = group_of(i)
    if group == "Y":
        return EXTRA_BASE[half], EXTRA[half]
    if group == "X":
        return PAIR_BASE[half] + START[half]["MX"], ROWS[half] - START[half]["MX"]
    return None


def additions_of(i):
    half, group, place = group_of(i)
    other = 1 - half
    apart, within = [], []
    for g, (first, _) in HALVES[half].items():
        for chunk, row, step, at, count in rows_with(half, (group, place), g):
            a = first + at - FIRST[half]
            if half == 0:
                source, steps = a * COUNT[1], (COUNT[1], 1)
            else:
                source, steps = a, (1, COUNT[1])
            out = within if g == group else apart
            out.append((source, [(steps[0], count), (steps[1], COUNT[other])],
                        chunk, slot_of(chunk, FIRST[other]), row, [(0, step), (1, 0)]))
    x, m, y = (HALVES[half][g] for g in "XMY")
    start = START[half]
    one, two = 2 * half, 2 * half + 1
    if group == "Y":
        x_by_x = CROSS + x[1] * y[1]
        m_by_m = x_by_x + x[1] * x[1]
        my = start["MY"] - CHUNKS[two]["lo"] + place
        if SQUARE_M[half]:
            apart.append((m_by_m, [(m[1], m[1]), (1, m[1])],
                          two, slot_of(two, m[0]), my, [(0, y[1]), (1, 0)]))
        else:
            for j in range(m[1]):
                apart.append((m_by_m + tri(m[1], j), [(1, m[1] - j)],
                              two, slot_of(two, m[0] + j), my + j * y[1], [(1, 0)]))
        apart.append((x_by_x, [(x[1], x[1]), (1, x[1])],
                      one, slot_of(one, x[0]), start["XY"] + place, [(0, y[1]), (1, 0)]))
        for chunk, row, step, at, count in rows_with(half, ("Y", place), "Y"):
            within.append((CROSS + at, [(y[1], x[1]), (1, count)],
                           chunk, slot_of(chunk, x[0]), row, [(1, 0), (0, step)]))
    if group == "X":
        extra = CROSS - start["MX"]
        apart.append((extra + start["MY"], [(y[1], m[1]), (1, y[1])],
                      one, slot_of(one, m[0]), start["XY"] + place * y[1], [(1, 0), (0, 1)]))
        for chunk, row, step, at, count in rows_with(half, ("X", place), "X"):
            within.append((extra + start["MX"] + at, [(x[1], m[1]), (1, count)],
                           chunk, slot_of(chunk, m[0]), row, [(1, 0), (0, step)]))
    return apart, within


def together(i):
    return i % 2 == 0 and i + 1 < FEATURES and group_of(i)[:2] == group_of(i + 1)[:2]


def build(nc, args):
    import concourse.bass as bass
    from concourse import mybir
    from contextlib import ExitStack

    FP = mybir.dt.float32
    ALU = mybir.AluOpType
    ACT = mybir.ActivationFunctionType

    ctx = ExitStack()
    with ctx:
        def sb(name, shape, dt=FP):
            return ctx.enter_context(nc.sbuf_tensor(name, shape, dt))

        def sem(name):
            return ctx.enter_context(nc.semaphore(name))

        SLOTS = len(CHUNKS) * WINDOW
        shared = sb("shared", [128, SLOTS * 128])
        weights_h = shared[:, :].rearrange("h (s r) -> h s r", r=128)
        products = [shared[:, n * 4096:(n + 1) * 4096].rearrange("p (b r) -> p b r", r=128) for n in range(2)]
        moments = [shared[:, (2 + n) * 4096:(3 + n) * 4096].rearrange("r (c q) -> r c q", c=WINDOW) for n in range(2)]
        weights = sb("weights", [128, SLOTS, 128])
        pair_w = [weights[:, PAIR_TILES * n:PAIR_TILES * (n + 1), :] for n in range(2)]
        pair_sum = weights[:, 2 * PAIR_TILES:3 * PAIR_TILES, :]
        w1 = sb("w1", [128, FEATURES * 128])
        z1_w = w1[:, 0:TILES * 128].rearrange("p (t h) -> p t h", h=128)
        second = w1[:, TILES * 128:2 * TILES * 128].rearrange("p (t s) -> p t s", s=128)
        z = w1[:, 2 * TILES * 128:2 * TILES * 128 + 2 * BATCH]
        rows_in = sb("rows_in", [128, FEATURES * DIM])
        xt = sb("xt", [128, 2, FEATURES, SUB])
        squares_all = sb("squares", [128, FEATURES * DIM])
        squares = squares_all[:, :].rearrange("p (h f i) -> p h f i", h=2, i=SUB)
        first_squares = weights[:, SLOTS // 2:, :].rearrange("p s h -> p (s h)")[:, 0:FEATURES * DIM].rearrange(
            "p (h f i) -> p h f i", h=2, i=SUB)
        pair_t = squares_all[:, 0:PAIR_COLS]
        z1_sum = squares_all[:, PAIR_COLS:PAIR_COLS + TILES * 128].rearrange("p (t h) -> p t h", h=128)
        z1_part = weights[:, 3 * PAIR_TILES:3 * PAIR_TILES + TILES, :]
        xd = sb("xd", [128, HALF, 2, WRAPPED])
        ids_now = sb("ids_now", [128, FEATURES], mybir.dt.int32)
        gate = sb("gate", [128, 2])
        ident = sb("ident", [128, 128])
        top1_w = rows_in[:, 0:2 * TOP1].rearrange("p (t n) -> p t n", n=TOP1)
        top1_wd = squares_all[0:16, 0:TOP1]
        top2_w = rows_in[:, 2 * TOP1:2 * TOP1 + 4 * TOP2].rearrange("p (t n) -> p t n", n=TOP2)
        hidden1 = xt[:, :, :, :].rearrange("p s f i -> p (s f i)")[:, 0:4 * BATCH].rearrange("p (t s) -> p t s", s=BATCH)
        xd_flat = xd[:, :, :, :].rearrange("p b q f -> p (b q f)")
        hidden2 = xd_flat[:, 0:2 * BATCH].rearrange("p (t s) -> p t s", s=BATCH)
        dense = xd_flat[0:16, 2 * BATCH:3 * BATCH]
        answer = xd_flat[0:1, 3 * BATCH:4 * BATCH]
        columns = xd_flat[:, 4 * BATCH:4 * BATCH + 8]
        banks = ctx.enter_context(nc.psum_tensor("banks", [128, 8 * 512], FP))
        bank = [banks[:, 512 * n:512 * (n + 1)] for n in range(8)]
        ring, turn_banks, z2_bank, z1_bank = bank[0:4], bank[4:8], bank[6], bank[7]

        w0_loaded = [sem(f"w0_loaded{n}") for n in range(2)]
        w1_loaded = [sem(f"w1_loaded{n}") for n in range(4)]
        first_ids_loaded = sem("first_ids_loaded")
        ids_loaded = sem("ids_loaded")
        z1w_loaded = sem("z1w_loaded")
        z1w_moved = sem("z1w_moved")
        top_loaded = sem("top_loaded")
        second_loaded = [sem(f"second_loaded{c}") for c in range(4)]
        answer_stored = sem("answer_stored")
        ident_set = sem("ident_set")
        gate_passed = sem("gate_passed")
        xd_zeroed = sem("xd_zeroed")
        places_zeroed = sem("places_zeroed")
        gathered = sem("gathered")
        pairs_summed = sem("pairs_summed")
        pairs_flipped = sem("pairs_flipped")
        pairs_ready = sem("pairs_ready")
        direct_a = sem("direct_a")
        direct_b = sem("direct_b")
        placed_a = [sem("placed_a_even"), sem("placed_a_odd")]
        placed_b = sem("placed_b")
        extra_done = sem("extra_done")
        added = sem("added")
        turned = sem("turned")
        kept = sem("kept")
        rows_turned = sem("rows_turned")
        rows_moved = sem("rows_moved")
        xd_ready = sem("xd_ready")
        products_ready = sem("products_ready")
        moments_out = sem("moments_out")
        moments_ready = sem("moments_ready")
        moments_freed = sem("moments_freed")
        z1w_ready = sem("z1w_ready")
        z1_done = sem("z1_done")
        z_kept = sem("z_kept")
        top_done = sem("top_done")
        top_kept = sem("top_kept")

        CHUNK_TILES = [sum(t[0] == chunk for t in MOMENT_TILES) for chunk in range(4)]
        C_BANKS = SLOTS // 4
        HALF_BANKS = C_BANKS // 2
        EVEN, ODD = (FEATURES + 1) // 2, FEATURES // 2
        W1_PIECE = -(-FEATURES // len(w1_loaded))
        TURN_AT = 25
        ROWS_AT = 16
        WARM_UPS = 8
        MOVES = 8
        GROUPS = HALF // GROUP
        SUB_GROUPS = GROUPS // 2
        BLOCK_GROUPS = len(CHUNKS) * GROUPS
        RING = len(ring)
        FREE_GROUPS = 2 * SUB_GROUPS

        def place_direct(op, tail, i, half, done):
            source = bank[4 * half + i % 4]
            moves = []
            one, two = 2 * half, 2 * half + 1
            if slot_of(one, i) is not None:
                moves.append((one, 0, START[half]["MX"]))
            if slot_of(two, i) is not None:
                own_y = group_of(i)[:2] == (half, "Y")
                moves.append((two, START[half]["YY" if own_y else "MX"], ROWS[half]))
            for n, (chunk, lo, hi) in enumerate(moves):
                row = lo - CHUNKS[chunk]["lo"]
                ins = op(weights_h[:, WINDOW * chunk + slot_of(chunk, i), row:row + hi - lo],
                         source[:, lo:hi], *tail)
                if n == len(moves) - 1:
                    ins.then_inc(done, 1)

        def piece_of_xd(n):
            return xd[:, 8 * n:8 * n + 8, :, :].rearrange("p b q f -> p (b q f)")

        def ap_of(base, offset, axes):
            return bass.AP(base.tensor, base.offset + offset, [list(base.ap[0])] + [list(a) for a in axes])

        block = ctx.enter_context(nc.Block())

        @block.sync
        def _(sp):
            def load_pairs(n):
                tiles = slice(4 * n, min(4 * n + 4, PAIR_TILES))
                for to, name in zip(pair_w, ("pairs_a", "pairs_b")):
                    rows = args[name].rearrange("(t p) h -> p t h", p=128)
                    sp.dma_start(to[:, tiles, :], rows[:, tiles, :]).then_inc(w0_loaded[n], 16)

            def load_w1(n):
                cols = slice(128 * W1_PIECE * n, min(128 * W1_PIECE * (n + 1), 128 * FEATURES))
                sp.dma_start(w1[:, cols], args["w1"][:, cols]).then_inc(w1_loaded[n], 16)

            sp.dma_start(ids_now[:, :], args["ids"][0:BLOCK, :]).then_inc(first_ids_loaded, 16)
            load_pairs(0)
            load_w1(0)
            load_pairs(1)
            for n in range(1, len(w1_loaded)):
                load_w1(n)
            sp.dma_start(z1_sum, args["z1_a"].rearrange("t p h -> p t h")).then_inc(z1w_loaded, 16)
            sp.dma_start(z1_part, args["z1_b"].rearrange("t p h -> p t h")).then_inc(z1w_loaded, 16)

            def move_rows(source):
                for q in range(2):
                    for e in range(2):
                        for h in range(2):
                            of, to = 64 * q + 32 * e, 64 * q + 32 * h
                            sp.dma_start(xt[to:to + 32, e], source[of:of + 32, h]).then_inc(rows_moved, 16)

            def move_second(k, chunk):
                sp.wait_ge(moments_ready, RING + BLOCK_GROUPS * k + GROUPS * (chunk + 1))
                for t, (of, row, n, slot, slots) in enumerate(MOMENT_TILES):
                    if of == chunk:
                        src = moments[chunk % 2][row:row + n, slot:slot + slots, :]
                        sp.dma_start(second[0:n * slots, t, :], src).then_inc(second_loaded[chunk], 16)

            def moves(k, last_one):
                sp.wait_ge(z_kept, 2 * (k + 1))
                move_second(k, 1)
                move_second(k, 2)
                if not last_one:
                    sp.wait_ge(rows_turned, 2 * (k + 2))
                    move_rows(squares)
                move_second(k, 3)

            sp.wait_ge(rows_turned, 2)
            move_rows(first_squares)
            sp.wait_ge(z1w_ready, 1)
            sp.wait_ge(extra_done, FEATURES)
            sp.dma_start(z1_w, z1_sum).then_inc(z1w_moved, 16)
            with sp.Fori(0, BLOCKS - 1) as k:
                moves(k, False)
            moves(BLOCKS - 1, True)
            sp.wait_ge(rows_turned, 2 * BLOCKS)
            sp.dma_start(top1_w, args["W_top1"][0:256, :].rearrange("(t p) n -> p t n", p=128)).then_inc(top_loaded, 16)
            sp.wait_ge(rows_moved, 16 * MOVES * BLOCKS)
            sp.dma_start(top1_wd, args["W_top1"][256:272, :]).then_inc(top_loaded, 16)
            sp.dma_start(top2_w, args["W_top2"].rearrange("(t p) n -> p t n", p=128)).then_inc(top_loaded, 16)
            sp.wait_ge(moments_out, FREE_GROUPS + BLOCK_GROUPS * BLOCKS)
            sp.dma_start(dense, args["dense_t"]).then_inc(top_loaded, 16)
            sp.dma_start(columns, args["columns"]).then_inc(top_loaded, 16)
            sp.wait_ge(top_kept, 7)
            sp.dma_start(args["out"].rearrange("s o -> o s"), answer).then_inc(answer_stored, 16)
            sp.wait_ge(answer_stored, 16)

        @block.gpsimd
        def _(pool):
            pool.memset(gate[:, :], 0.0).then_inc(gate_passed, 1)
            pool.memset(ident[:, :], 1.0).then_inc(ident_set, 1)
            pool.wait_ge(ident_set, 1)
            pool.affine_select(out=ident[:, :], in_=ident[:, :], compare_op=ALU.is_equal, fill=0.0,
                               base=0, pattern=[[-1, 128]], channel_multiplier=1).then_inc(ident_set, 1)

            def gather(k):
                if isinstance(k, int):
                    pool.wait_ge(first_ids_loaded, 16)
                else:
                    pool.wait_ge(gate_passed, k)
                    pool.wait_ge(rows_turned, 2 * k)
                    pool.dma_start(ids_now[:, :], args["ids"][bass.ts(k, BLOCK), :]).then_inc(ids_loaded, 16)
                    pool.wait_ge(ids_loaded, 16 * k)
                    pool.tensor_tensor(gate[:, 1:2], gate[:, 0:1], gate[:, 0:1], ALU.add).then_inc(gate_passed, 1)
                for f in range(FEATURES):
                    pool.indirect_dma_start(
                        rows_in[:, f * DIM:(f + 1) * DIM], None, args[f"tbl_{f}"],
                        bass.IndirectOffsetOnAxis(ap=ids_now[:, f:f + 1], axis=0)).then_inc(gathered, 16)

            gather(0)
            with pool.Fori(0, BLOCKS - 1) as k:
                gather(k + 1)

        @block.scalar
        def _(act):
            def pairs_out(n):
                act.wait_ge(pairs_flipped, n + 1)
                for lo, hi in ((0, ROWS[0]), (ROWS[0], 512)) if n == 0 else ((512, PAIR_COLS),):
                    act.activation(pair_t[:, lo:hi], bank[6 + n][:, lo - 512 * n:hi - 512 * n], ACT.Copy).then_inc(pairs_ready, 1)

            pairs_out(0)
            act.wait_ge(places_zeroed, 1)
            for i in range(0, FEATURES, 2):
                if i == 4:
                    pairs_out(1)
                act.wait_ge(direct_a, i + 1)
                place_direct(act.activation, (ACT.Copy,), i, 0, placed_a[0])
                if i == 4:
                    act.wait_ge(gate_passed, 1)
                if 4 <= i < 20 and i % 4 == 0:
                    piece = piece_of_xd(i // 4 + 3)
                    act.activation(piece, gate[:, 0:1].to_broadcast(list(piece.shape)), ACT.Copy).then_inc(xd_zeroed, 1)

            def spread(n):
                f, to, count = ((20, 20, 19), (0, 39, 13), (0, 0, 20), (13, 52, 7))[n // 2]
                q = n % 2
                of = slice(64 * q, 64 * q + 64)
                out = xd[of, :, q, to:to + count].rearrange("p (s i) f -> p s i f", i=SUB)
                rows = xt[of, :, f:f + count, :].rearrange("p s f i -> p s i f")
                act.activation(out, rows, ACT.Copy).then_inc(xd_ready, 1)

            for i in range(FEATURES):
                act.wait_ge(direct_b, i + 1)
                place_direct(act.activation, (ACT.Copy,), i, 1, placed_b)
            act.wait_ge(rows_moved, 16 * MOVES)
            act.wait_ge(xd_zeroed, 8)
            for n in range(4):
                spread(n)

            def keep(v):
                act.wait_ge(turned, v + 1)
                act.activation(weights[:, 4 * v:4 * v + 4, :].rearrange("r s h -> r (s h)"),
                               turn_banks[v % 4][:, :], ACT.Copy).then_inc(kept, 1)

            act.wait_ge(z1w_ready, 1)
            for v in range(C_BANKS):
                keep(v)
                if v < 12 and v % 3 == 2:
                    spread(4 + v // 3)

            def chunk_out(k, chunk):
                act.wait_ge(moments_freed, 4 * k + chunk + 1)
                if chunk == 3:
                    act.wait_ge(second_loaded[1], 16 * CHUNK_TILES[1] * (k + 1))
                n = CHUNK_ROWS[chunk]
                out = moments[chunk % 2].rearrange("r c (q b) -> r c q b", q=2)
                for g in range(GROUPS):
                    act.wait_ge(moments_out, FREE_GROUPS + BLOCK_GROUPS * k + GROUPS * chunk + g + 1)
                    act.activation(out[0:n, :, :, GROUP * g:GROUP * (g + 1)],
                                   ring[g % 4][0:n, :].rearrange("r (b q c) -> r c q b", b=GROUP, q=2),
                                   ACT.Copy).then_inc(moments_ready, 1)

            def block_out(k, last):
                chunk_out(k, 1)
                chunk_out(k, 2)
                chunk_out(k, 3)
                if not last:
                    act.wait_ge(moments_out, FREE_GROUPS + BLOCK_GROUPS * (k + 1))
                    act.wait_ge(rows_moved, 16 * MOVES * (k + 2))
                    for n in range(8):
                        spread(n)
                    act.wait_ge(second_loaded[2], 16 * CHUNK_TILES[2] * (k + 1))
                    chunk_out(k + 1, 0)
                act.wait_ge(moments_freed, 2 + 4 * (k + 1))
                act.activation(z[:, bass.ds(BATCH + BLOCK * k, BLOCK)], z2_bank[:, 0:BLOCK], ACT.Copy).then_inc(z_kept, 1)
                act.wait_ge(z1_done, k + 1)
                act.activation(z[:, bass.ds(BLOCK * k, BLOCK)], z1_bank[:, 0:BLOCK], ACT.Copy).then_inc(z_kept, 1)

            chunk_out(0, 0)
            with act.Fori(0, BLOCKS - 1) as k:
                block_out(k, False)
            block_out(BLOCKS - 1, True)
            act.wait_ge(top_loaded, 80)
            for t in range(4):
                act.wait_ge(top_done, t + 1)
                act.activation(hidden1[:, t, :], ring[t][:, :], ACT.Relu, bias=columns[:, t:t + 1]).then_inc(top_kept, 1)
            for t in range(2):
                act.wait_ge(top_done, t + 5)
                act.activation(hidden2[:, t, :], turn_banks[t][:, :], ACT.Relu, bias=columns[:, 4 + t:5 + t]).then_inc(top_kept, 1)
            act.wait_ge(top_done, 7)
            act.activation(answer, z1_bank[0:1, :], ACT.Copy).then_inc(top_kept, 1)

        @block.vector
        def _(dve):
            for chunk in range(4):
                nc.vector.memset(weights_h[:, WINDOW * chunk:WINDOW * (chunk + 1), PAIR_ROWS[chunk]:], 0.0)
            for half in (0, 1):
                two = 2 * half + 1
                first = slot_of(two, HALVES[half]["Y"][0])
                yy = START[half]["MX"] - START[half]["YY"]
                for lo, hi in ((0, first), (first + 7, WINDOW)):
                    if hi > lo:
                        last = nc.vector.memset(weights_h[:, WINDOW * two + lo:WINDOW * two + hi, 0:yy], 0.0)
            last.then_inc(places_zeroed, 1)
            for n, loaded in enumerate(w0_loaded):
                dve.wait_ge(loaded, 32)
                tiles = slice(4 * n, min(4 * n + 4, PAIR_TILES))
                nc.vector.tensor_tensor(pair_sum[:, tiles, :], pair_w[0][:, tiles, :], pair_w[1][:, tiles, :],
                                        ALU.add).then_inc(pairs_summed, 1)
            for i in range(1, FEATURES, 2):
                dve.wait_ge(direct_a, i + 1)
                place_direct(nc.vector.tensor_copy, (), i, 0, placed_a[1])
                if 5 <= i < 21 and i % 4 == 1:
                    nc.vector.memset(piece_of_xd(i // 4 - 1), 0.0).then_inc(xd_zeroed, 1)
            dve.wait_ge(z1w_loaded, 32)
            nc.vector.tensor_tensor(z1_sum, z1_sum, z1_part, ALU.add).then_inc(z1w_ready, 1)

            def turn_rows(k, out):
                dve.wait_ge(gathered, 16 * FEATURES * (k + 1))
                rows = rows_in[:, :].rearrange("p (f h i) -> p h f i", h=2, i=SUB)
                for h in range(2):
                    nc.vector.transpose(out[:, h], rows[:, h]).then_inc(rows_turned, 1)

            for i in range(FEATURES):
                if i == ROWS_AT:
                    turn_rows(0, first_squares)
                dve.wait_ge(extra_done, i + 1)
                if i == 0:
                    dve.wait_ge(placed_a[0], EVEN)
                    dve.wait_ge(placed_a[1], ODD)
                if i == FIRST[1]:
                    dve.wait_ge(placed_b, FEATURES)
                apart, within = additions_of(i)
                if i % 2 and together(i - 1):
                    apart = []
                two = together(i)
                if two:
                    dve.wait_ge(extra_done, i + 2)
                if i and not group_of(i)[2]:
                    dve.wait_ge(added, i)
                for n, (col, axes, chunk, slot, row, steps) in enumerate(apart):
                    source = list(axes)
                    place = [(128 * s + r, count) for (s, r), (_, count) in zip(steps, axes)]
                    if two:
                        source.insert(0, (512, 2))
                        place.insert(0, (additions_of(i + 1)[0][n][4] - row, 2))
                    place = ap_of(shared[:, :], (WINDOW * chunk + slot) * 128 + row, place)
                    nc.vector.tensor_tensor(place, ap_of(ring[i % 4], col, source), place, ALU.add)
                if i and group_of(i)[2]:
                    dve.wait_ge(added, i)
                for col, axes, chunk, slot, row, steps in within:
                    place = ap_of(shared[:, :], (WINDOW * chunk + slot) * 128 + row,
                                  [(128 * s + r, count) for (s, r), (_, count) in zip(steps, axes)])
                    ins = nc.vector.tensor_tensor(place, ap_of(ring[i % 4], col, axes), place, ALU.add)
                ins.then_inc(added, 1)

            def multiply(k):
                dve.wait_ge(rows_moved, 16 * MOVES * (k + 1))
                for chunk in range(4):
                    for s in range(2):
                        dve.wait_ge(moments_out, SUB_GROUPS * (8 * k + 2 * chunk + s + 1))
                        x = xt[:, s]
                        own, count = CHUNKS[chunk]["own"]
                        if count:
                            row = PAIR_ROWS[chunk]
                            nc.vector.tensor_copy(products[s][:, :, row:row + count],
                                                  x[:, own:own + count, :].rearrange("p f b -> p b f"))
                        for row, fa, na, fb, nb, slide in pieces_of_chunk(chunk):
                            out = products[s][:, :, row:row + na * nb].rearrange("p b (i j) -> p b i j", i=na)
                            one, two = x[:, fa:fa + na, :], x[:, fb:fb + nb, :]
                            one = one.rearrange("p (f o) b -> p b f o", o=1).to_broadcast([128, SUB, na, nb])
                            if slide:
                                two = ap_of(x[:, fb:fb + nb, :], 0, [(1, SUB), (SUB, na), (SUB, nb)])
                            else:
                                two = two.rearrange("p (o f) b -> p b o f", o=1).to_broadcast([128, SUB, na, nb])
                            last = nc.vector.tensor_tensor(out, one, two, ALU.mult)
                        last.then_inc(products_ready, 1)

            multiply(0)
            with dve.Fori(0, BLOCKS - 1) as k:
                turn_rows(k + 1, squares)
                multiply(k + 1)

        @block.tensor
        def _(pe):
            pe.wait_ge(ident_set, 2)
            for _ in range(WARM_UPS):
                nc.tensor.matmul(bank[5][:, 0:128], ident[:, :], ident[:, :], start=True, stop=True)

            def turn_pairs(n):
                pe.wait_ge(pairs_summed, n + 1)
                for t in range(4 * n, min(4 * n + 4, PAIR_TILES)):
                    cols = min(128, PAIR_COLS - 128 * t)
                    last = nc.tensor.transpose(bank[6 + n][:, 128 * (t % 4):128 * (t % 4) + cols],
                                               pair_sum[0:cols, t, :], ident[0:cols, 0:cols])
                last.then_inc(pairs_flipped, 1)

            turn_pairs(0)
            pe.wait_ge(pairs_ready, 1)

            def direct(i, half, done):
                col = PAIR_BASE[half]
                nc.tensor.matmul(bank[4 * half + i % 4][:, 0:ROWS[half]], w1[:, 128 * i:128 * (i + 1)],
                                 pair_t[:, col:col + ROWS[half]], start=True, stop=True).then_inc(done, 1)

            for i in range(FEATURES):
                if i % W1_PIECE == 0:
                    pe.wait_ge(w1_loaded[i // W1_PIECE], 16)
                if i == 3:
                    turn_pairs(1)
                if i >= 4:
                    pe.wait_ge(placed_a[i % 2], i // 2 - 1)
                direct(i, 0, direct_a)

            def turn(v):
                if v >= 4:
                    pe.wait_ge(kept, v - 3)
                out = turn_banks[v % 4]
                for s in range(4):
                    last = nc.tensor.transpose(out[:, 128 * s:128 * (s + 1)], weights_h[:, 4 * v + s, :], ident[:, :])
                last.then_inc(turned, 1)

            pe.wait_ge(pairs_ready, 3)
            direct(0, 1, direct_b)
            direct(1, 1, direct_b)
            pe.wait_ge(placed_a[0], EVEN)
            pe.wait_ge(placed_a[1], ODD)
            for i in range(FEATURES):
                if i >= 4:
                    pe.wait_ge(added, i - 3)
                extra = extra_of(i)
                w = w1[:, 128 * i:128 * (i + 1)]
                last = nc.tensor.matmul(ring[i % 4][:, 0:CROSS], w, pair_t[:, PAIRS:PAIRS + CROSS], start=True, stop=True)
                if extra:
                    col, n = extra
                    last = nc.tensor.matmul(ring[i % 4][:, CROSS:CROSS + n], w, pair_t[:, col:col + n],
                                            start=True, stop=True)
                last.then_inc(extra_done, 1)
                for f in (i - 1, i) if i % 2 else (i,) if i == FEATURES - 1 else ():
                    for j in range(max(2 * f, 2), min(2 * f + 2, FEATURES)):
                        if j >= 4:
                            pe.wait_ge(placed_b, j - 3)
                        direct(j, 1, direct_b)
                    if f == TURN_AT:
                        pe.wait_ge(added, FIRST[1])
                        pe.wait_ge(placed_b, FEATURES)
                    if f >= TURN_AT:
                        turn(f - TURN_AT)
            for v in range(FEATURES - TURN_AT, HALF_BANKS):
                turn(v)
            pe.wait_ge(kept, HALF_BANKS - 3)
            nc.tensor.matmul(turn_banks[0][0:1, 0:1], ident[:, 0:1], ident[:, 0:1], start=True, stop=True).then_inc(moments_out, FREE_GROUPS)
            pe.wait_ge(added, FEATURES)
            for v in range(HALF_BANKS, C_BANKS):
                turn(v)
            nc.tensor.matmul(ring[0][0:1, 0:1], ident[:, 0:1], ident[:, 0:1], start=True, stop=True).then_inc(moments_freed, 2)
            nc.tensor.matmul(ring[0][0:1, 0:1], ident[:, 0:1], ident[:, 0:1], start=True, stop=True).then_inc(moments_ready, RING)

            def take_moments(k, chunk):
                n, window = CHUNK_ROWS[chunk], CHUNKS[chunk]["window"]
                for g in range(GROUPS):
                    s, q = divmod(g, SUB_GROUPS)
                    if q == 0:
                        pe.wait_ge(products_ready, 8 * k + 2 * chunk + s + 1)
                    pe.wait_ge(moments_ready, BLOCK_GROUPS * k + GROUPS * chunk + g + 1)
                    for j in range(GROUP):
                        for lo, hi in ((0, 64), (64, n)):
                            out = ring[g % 4][lo:hi, 64 * j:64 * (j + 1)].rearrange("r (q c) -> r q c", q=2)
                            last = nc.tensor.matmul(out, products[s][:, GROUP * q + j, lo:hi],
                                                    xd[:, GROUP * g + j, :, window:window + WINDOW], start=True, stop=True)
                    last.then_inc(moments_out, 1)

            def weigh(k, chunk):
                n = CHUNK_ROWS[chunk]
                pe.wait_ge(moments_ready, RING + BLOCK_GROUPS * k + GROUPS * (chunk + 1))
                if chunk == 0:
                    pe.wait_ge(z_kept, 2 * (k + 1))
                for c in range(WINDOW):
                    last = nc.tensor.matmul(z2_bank[:, 0:BLOCK], weights[0:n, WINDOW * chunk + c, :],
                                            moments[chunk % 2][0:n, c, :],
                                            start=(chunk == 0 and c == 0), stop=(chunk == 3 and c == WINDOW - 1))
                last.then_inc(moments_freed, 1)

            def whole_block(k, last_one):
                pe.wait_ge(xd_ready, 8 * (k + 1))
                take_moments(k, 1)
                weigh(k, 0)
                take_moments(k, 2)
                weigh(k, 1)
                take_moments(k, 3)
                weigh(k, 2)
                if not last_one:
                    pe.wait_ge(xd_ready, 8 * (k + 1) + 4)
                    take_moments(k + 1, 0)
                weigh(k, 3)
                for chunk in (1, 2, 3):
                    pe.wait_ge(second_loaded[chunk], 16 * CHUNK_TILES[chunk] * (k + 1))
                for t, (_, _, n, _, slots) in enumerate(MOMENT_TILES):
                    last = nc.tensor.matmul(z1_bank[:, 0:BLOCK], z1_w[0:n * slots, t, :], second[0:n * slots, t, :],
                                            start=(t == 0), stop=(t == TILES - 1))
                last.then_inc(z1_done, 1)

            pe.wait_ge(xd_ready, 4)
            take_moments(0, 0)
            pe.wait_ge(kept, C_BANKS)
            nc.tensor.matmul(z1_bank[0:1, 0:1], ident[:, 0:1], ident[:, 0:1], start=True, stop=True).then_inc(z_kept, 2)
            pe.wait_ge(z1w_moved, 16)
            with pe.Fori(0, BLOCKS - 1) as k:
                whole_block(k, False)
            whole_block(BLOCKS - 1, True)
            pe.wait_ge(top_loaded, 80)
            for t in range(4):
                cols = slice(128 * t, 128 * (t + 1))
                nc.tensor.matmul(ring[t][:, :], top1_wd[:, cols], dense, start=True, stop=False)
                if t == 0:
                    pe.wait_ge(z_kept, 2 + 2 * BLOCKS)
                nc.tensor.matmul(ring[t][:, :], top1_w[:, 0, cols], z[:, 0:BATCH], start=False, stop=False)
                nc.tensor.matmul(ring[t][:, :], top1_w[:, 1, cols], z[:, BATCH:2 * BATCH], start=False, stop=True).then_inc(top_done, 1)
            for s in range(4):
                pe.wait_ge(top_kept, s + 1)
                for t in range(2):
                    last = nc.tensor.matmul(turn_banks[t][:, :], top2_w[:, s, 128 * t:128 * (t + 1)], hidden1[:, s, :],
                                            start=(s == 0), stop=(s == 3))
                    if s == 3:
                        last.then_inc(top_done, 1)
            for s in range(2):
                pe.wait_ge(top_kept, 5 + s)
                last = nc.tensor.matmul(z1_bank[0:1, :], columns[:, 6 + s:7 + s], hidden2[:, s, :], start=(s == 0), stop=(s == 1))
            last.then_inc(top_done, 1)


def pair_index():
    zero = FEATURES * FEATURES
    pairs = pair_features(0) + pair_features(1)
    pairs += [(a, b) for a in range(COUNT[0]) for b in range(FIRST[1], FEATURES)]
    pairs = [(a, b, True) for a, b in pairs] + extra_pairs(0) + extra_pairs(1)
    one = [a * FEATURES + b for a, b, _ in pairs]
    two = [b * FEATURES + a if both and a != b else zero for a, b, both in pairs]
    fill = [zero] * (-len(pairs) % 128)
    return one + fill, two + fill


def moment_index():
    zero = FEATURES * FEATURES
    one, two = [], []
    for chunk, row, n, slot, slots in MOMENT_TILES:
        rows_one, rows_two = [], []
        for r in range(row, row + n):
            x = CHUNKS[chunk]["own"][0] + r - PAIR_ROWS[chunk]
            for s in range(slot, slot + slots):
                f = (CHUNKS[chunk]["window"] + s) % FEATURES
                rows_one.append(x * FEATURES + f)
                both = chunk == 3 and not (x < FIRST[1] and f < FIRST[1])
                rows_two.append(f * FEATURES + x if both else zero)
        fill = [zero] * (128 - n * slots)
        one += rows_one + fill
        two += rows_two + fill
    return one, two


def kernel(**inputs):
    import numpy as np
    import concourse.bacc as bacc
    from concourse import mybir
    from concourse.bass_utils import run_bass_kernel_spmd as run

    nc = bacc.Bacc("TRN2", target_bir_lowering=False, num_devices=1)
    w0 = np.asarray(inputs["L0_rec_W0"]).reshape(FEATURES * FEATURES, HID)
    w0 = np.concatenate([w0, np.zeros((1, HID), w0.dtype)])
    pairs_a, pairs_b = pair_index()
    z1_a, z1_b = moment_index()
    arrays = {
        "ids": inputs["ids"],
        "pairs_a": w0[np.array(pairs_a)],
        "pairs_b": w0[np.array(pairs_b)],
        "z1_a": w0[np.array(z1_a)].reshape(TILES, 128, HID),
        "z1_b": w0[np.array(z1_b)].reshape(TILES, 128, HID),
        "w1": np.asarray(inputs["L0_rec_W1"]).transpose(1, 0, 2).reshape(HID, FEATURES * HID),
        "dense_t": np.asarray(inputs["dense_ctx"]).T,
        "W_top1": inputs["W_top1"],
        "W_top2": inputs["W_top2"],
        "columns": np.concatenate([np.asarray(inputs[n]).reshape(-1, 128) for n in ("b_top1", "b_top2", "W_top3")]).T,
    }
    arrays.update({f"tbl_{f}": inputs[f"tbl_{f}"] for f in range(FEATURES)})
    arrays = {f"in_{n}": np.ascontiguousarray(a) for n, a in arrays.items()}
    args = {n[3:]: nc.dram_tensor(n, a.shape, mybir.dt.from_np(a.dtype), kind="ExternalInput").ap()
            for n, a in arrays.items()}
    args["out"] = nc.dram_tensor("out", (BATCH, 1), mybir.dt.float32, kind="ExternalOutput").ap()
    build(nc, args)
    return run(nc, [arrays], core_ids=[0]).results[0]["out"]
```
